# Optimizing a Trainium2 kernel written in Bass

```python
import numpy as np
import jax
import jax.numpy as jnp

def _softmax(x, axis=-1):
    return jax.nn.softmax(x, axis=axis)

def _gelu(x):
    return jax.nn.gelu(x, approximate=True)

def _silu(x):
    return jax.nn.silu(x)

def _sigmoid(x):
    return jax.nn.sigmoid(x)

def _layernorm(x, axis=-1, eps=1e-05):
    m = jnp.mean(x, axis=axis, keepdims=True)
    v = jnp.var(x, axis=axis, keepdims=True)
    return (x - m) / jnp.sqrt(v + eps)

def _scatter_add(tgt, idx, src, axis=0):
    return tgt.at[idx].add(src)

def _segment_sum(src, seg, n):
    return jax.ops.segment_sum(src, seg, n)
kernel_name = 'mk_dlrm_tower_d1_rec_r8_9a1bc7'

def setup_inputs(seed: int=0):
    np.random.seed(seed)
    _w = jnp.asarray

    def _rec_inputs():
        import jax
        import jax.numpy as jnp
        _tk = jax.random.key(seed)
        dense_ctx = jax.random.normal(jax.random.fold_in(_tk, 190), (1024, 16), jnp.float32)
        ids = jnp.stack([jax.random.randint(jax.random.fold_in(_tk, 200 + f), (1024,), 0, v, jnp.int32) for f, v in enumerate([125000, 12500, 125000, 1000, 1250, 1250, 1000, 12500, 12500, 125000, 12500, 1250, 12500, 12500, 125000, 125000, 1250, 1000, 12500, 12500, 12500, 125000, 1000, 1000, 125000, 125000, 1000, 1000, 1000, 125000, 1250, 1000])], axis=1)
        tbl_0 = 0.05 * jax.random.normal(jax.random.fold_in(_tk, 500 + 0), (125000, 16), jnp.float32)
        tbl_1 = 0.05 * jax.random.normal(jax.random.fold_in(_tk, 500 + 1), (12500, 16), jnp.float32)
        tbl_2 = 0.05 * jax.random.normal(jax.random.fold_in(_tk, 500 + 2), (125000, 16), jnp.float32)
        tbl_3 = 0.05 * jax.random.normal(jax.random.fold_in(_tk, 500 + 3), (1000, 16), jnp.float32)
        tbl_4 = 0.05 * jax.random.normal(jax.random.fold_in(_tk, 500 + 4), (1250, 16), jnp.float32)
        tbl_5 = 0.05 * jax.random.normal(jax.random.fold_in(_tk, 500 + 5), (1250, 16), jnp.float32)
        tbl_6 = 0.05 * jax.random.normal(jax.random.fold_in(_tk, 500 + 6), (1000, 16), jnp.float32)
        tbl_7 = 0.05 * jax.random.normal(jax.random.fold_in(_tk, 500 + 7), (12500, 16), jnp.float32)
        tbl_8 = 0.05 * jax.random.normal(jax.random.fold_in(_tk, 500 + 8), (12500, 16), jnp.float32)
        tbl_9 = 0.05 * jax.random.normal(jax.random.fold_in(_tk, 500 + 9), (125000, 16), jnp.float32)
        tbl_10 = 0.05 * jax.random.normal(jax.random.fold_in(_tk, 500 + 10), (12500, 16), jnp.float32)
        tbl_11 = 0.05 * jax.random.normal(jax.random.fold_in(_tk, 500 + 11), (1250, 16), jnp.float32)
        tbl_12 = 0.05 * jax.random.normal(jax.random.fold_in(_tk, 500 + 12), (12500, 16), jnp.float32)
        tbl_13 = 0.05 * jax.random.normal(jax.random.fold_in(_tk, 500 + 13), (12500, 16), jnp.float32)
        tbl_14 = 0.05 * jax.random.normal(jax.random.fold_in(_tk, 500 + 14), (125000, 16), jnp.float32)
        tbl_15 = 0.05 * jax.random.normal(jax.random.fold_in(_tk, 500 + 15), (125000, 16), jnp.float32)
        tbl_16 = 0.05 * jax.random.normal(jax.random.fold_in(_tk, 500 + 16), (1250, 16), jnp.float32)
        tbl_17 = 0.05 * jax.random.normal(jax.random.fold_in(_tk, 500 + 17), (1000, 16), jnp.float32)
        tbl_18 = 0.05 * jax.random.normal(jax.random.fold_in(_tk, 500 + 18), (12500, 16), jnp.float32)
        tbl_19 = 0.05 * jax.random.normal(jax.random.fold_in(_tk, 500 + 19), (12500, 16), jnp.float32)
        tbl_20 = 0.05 * jax.random.normal(jax.random.fold_in(_tk, 500 + 20), (12500, 16), jnp.float32)
        tbl_21 = 0.05 * jax.random.normal(jax.random.fold_in(_tk, 500 + 21), (125000, 16), jnp.float32)
        tbl_22 = 0.05 * jax.random.normal(jax.random.fold_in(_tk, 500 + 22), (1000, 16), jnp.float32)
        tbl_23 = 0.05 * jax.random.normal(jax.random.fold_in(_tk, 500 + 23), (1000, 16), jnp.float32)
        tbl_24 = 0.05 * jax.random.normal(jax.random.fold_in(_tk, 500 + 24), (125000, 16), jnp.float32)
        tbl_25 = 0.05 * jax.random.normal(jax.random.fold_in(_tk, 500 + 25), (125000, 16), jnp.float32)
        tbl_26 = 0.05 * jax.random.normal(jax.random.fold_in(_tk, 500 + 26), (1000, 16), jnp.float32)
        tbl_27 = 0.05 * jax.random.normal(jax.random.fold_in(_tk, 500 + 27), (1000, 16), jnp.float32)
        tbl_28 = 0.05 * jax.random.normal(jax.random.fold_in(_tk, 500 + 28), (1000, 16), jnp.float32)
        tbl_29 = 0.05 * jax.random.normal(jax.random.fold_in(_tk, 500 + 29), (125000, 16), jnp.float32)
        tbl_30 = 0.05 * jax.random.normal(jax.random.fold_in(_tk, 500 + 30), (1250, 16), jnp.float32)
        tbl_31 = 0.05 * jax.random.normal(jax.random.fold_in(_tk, 500 + 31), (1000, 16), jnp.float32)
        _rk = jax.random.fold_in(_tk, 7)
        W_top1 = 0.0693375 * jax.random.normal(jax.random.fold_in(_tk, 801), (208, 512), jnp.float32)
        W_top2 = 0.0441942 * jax.random.normal(jax.random.fold_in(_tk, 802), (512, 256), jnp.float32)
        W_top3 = 0.0625 * jax.random.normal(jax.random.fold_in(_tk, 803), (256, 1), jnp.float32)
        b_top1 = jnp.zeros((512,), jnp.float32)
        b_top2 = jnp.zeros((256,), jnp.float32)
        return (dense_ctx, ids, tbl_0, tbl_1, tbl_2, tbl_3, tbl_4, tbl_5, tbl_6, tbl_7, tbl_8, tbl_9, tbl_10, tbl_11, tbl_12, tbl_13, tbl_14, tbl_15, tbl_16, tbl_17, tbl_18, tbl_19, tbl_20, tbl_21, tbl_22, tbl_23, tbl_24, tbl_25, tbl_26, tbl_27, tbl_28, tbl_29, tbl_30, tbl_31, W_top1, b_top1, W_top2, b_top2, W_top3)
    dense_ctx, ids, tbl_0, tbl_1, tbl_2, tbl_3, tbl_4, tbl_5, tbl_6, tbl_7, tbl_8, tbl_9, tbl_10, tbl_11, tbl_12, tbl_13, tbl_14, tbl_15, tbl_16, tbl_17, tbl_18, tbl_19, tbl_20, tbl_21, tbl_22, tbl_23, tbl_24, tbl_25, tbl_26, tbl_27, tbl_28, tbl_29, tbl_30, tbl_31, W_top1, b_top1, W_top2, b_top2, W_top3 = _rec_inputs()

    def _L0_rec_setup():
        import jax, jax.numpy as jnp
        import numpy as np
        B, M, D = (2048, 32, 16)
        LAYERS = [64, 64, 64]
        key = jax.random.key(seed)
        ks = jax.random.split(key, 4)
        inp = {'embeddings': jax.random.normal(ks[0], (B, M, D), dtype=jnp.float32)}
        hk_1 = M
        for i, hk in enumerate(LAYERS):
            scale = (2.0 / (M * hk_1 + hk)) ** 0.5
            inp[f'W{i}'] = jax.random.normal(ks[i + 1], (M, hk_1, hk), dtype=jnp.float32) * scale
            hk_1 = hk
        return inp
    _L0_rec_all = _L0_rec_setup()
    _L0_rec_in = {k: v for k, v in _L0_rec_all.items() if k in ('W0', 'W1', 'W2')}
    del _L0_rec_all
    return {'dense_ctx': dense_ctx, 'ids': ids, 'tbl_0': tbl_0, 'tbl_1': tbl_1, 'tbl_2': tbl_2, 'tbl_3': tbl_3, 'tbl_4': tbl_4, 'tbl_5': tbl_5, 'tbl_6': tbl_6, 'tbl_7': tbl_7, 'tbl_8': tbl_8, 'tbl_9': tbl_9, 'tbl_10': tbl_10, 'tbl_11': tbl_11, 'tbl_12': tbl_12, 'tbl_13': tbl_13, 'tbl_14': tbl_14, 'tbl_15': tbl_15, 'tbl_16': tbl_16, 'tbl_17': tbl_17, 'tbl_18': tbl_18, 'tbl_19': tbl_19, 'tbl_20': tbl_20, 'tbl_21': tbl_21, 'tbl_22': tbl_22, 'tbl_23': tbl_23, 'tbl_24': tbl_24, 'tbl_25': tbl_25, 'tbl_26': tbl_26, 'tbl_27': tbl_27, 'tbl_28': tbl_28, 'tbl_29': tbl_29, 'tbl_30': tbl_30, 'tbl_31': tbl_31, 'W_top1': W_top1, 'b_top1': b_top1, 'W_top2': W_top2, 'b_top2': b_top2, 'W_top3': W_top3, 'L0_rec_W0': _L0_rec_in['W0'], 'L0_rec_W1': _L0_rec_in['W1'], 'L0_rec_W2': _L0_rec_in['W2']}

def reference(dense_ctx, ids, tbl_0, tbl_1, tbl_2, tbl_3, tbl_4, tbl_5, tbl_6, tbl_7, tbl_8, tbl_9, tbl_10, tbl_11, tbl_12, tbl_13, tbl_14, tbl_15, tbl_16, tbl_17, tbl_18, tbl_19, tbl_20, tbl_21, tbl_22, tbl_23, tbl_24, tbl_25, tbl_26, tbl_27, tbl_28, tbl_29, tbl_30, tbl_31, W_top1, b_top1, W_top2, b_top2, W_top3, L0_rec_W0, L0_rec_W1, L0_rec_W2):
    import jax
    import jax.numpy as jnp

    def _L0_rec_ref(embeddings, W0, W1, W2):
        import jax, jax.numpy as jnp
        import numpy as np
        B, M, D = (2048, 32, 16)
        LAYERS = [64, 64, 64]
        x0 = embeddings
        xk = x0
        outs = []
        for W in (W0, W1, W2):
            xk = jax.nn.relu(jnp.einsum('bmd,bhd,mhk->bkd', x0, xk, W))
            outs.append(jnp.sum(xk, axis=2))
        return jnp.concatenate(outs, axis=1)
    e = jnp.stack([tbl_0[ids[:, 0]], tbl_1[ids[:, 1]], tbl_2[ids[:, 2]], tbl_3[ids[:, 3]], tbl_4[ids[:, 4]], tbl_5[ids[:, 5]], tbl_6[ids[:, 6]], tbl_7[ids[:, 7]], tbl_8[ids[:, 8]], tbl_9[ids[:, 9]], tbl_10[ids[:, 10]], tbl_11[ids[:, 11]], tbl_12[ids[:, 12]], tbl_13[ids[:, 13]], tbl_14[ids[:, 14]], tbl_15[ids[:, 15]], tbl_16[ids[:, 16]], tbl_17[ids[:, 17]], tbl_18[ids[:, 18]], tbl_19[ids[:, 19]], tbl_20[ids[:, 20]], tbl_21[ids[:, 21]], tbl_22[ids[:, 22]], tbl_23[ids[:, 23]], tbl_24[ids[:, 24]], tbl_25[ids[:, 25]], tbl_26[ids[:, 26]], tbl_27[ids[:, 27]], tbl_28[ids[:, 28]], tbl_29[ids[:, 29]], tbl_30[ids[:, 30]], tbl_31[ids[:, 31]]], axis=1)
    z = _L0_rec_ref(e, L0_rec_W0, L0_rec_W1, L0_rec_W2)
    z = z.reshape(z.shape[0], -1)
    h = jnp.concatenate([z, dense_ctx], axis=1)
    h = jnp.maximum(h @ W_top1 + b_top1, 0.0)
    h = jnp.maximum(h @ W_top2 + b_top2, 0.0)
    y = h @ W_top3
    return y

_drawn_inputs = setup_inputs


def setup_inputs(seed=0):
    import zlib

    import numpy as np

    out = dict(_drawn_inputs(seed))
    spreads = {'b_top1': (0.0, 2.0), 'b_top2': (0.0, 0.8)}
    factors = {'tbl_0': 8.0,
     'tbl_1': 8.0,
     'tbl_2': 8.0,
     'tbl_3': 8.0,
     'tbl_4': 8.0,
     'tbl_5': 8.0,
     'tbl_6': 8.0,
     'tbl_7': 8.0,
     'tbl_8': 8.0,
     'tbl_9': 8.0,
     'tbl_10': 8.0,
     'tbl_11': 8.0,
     'tbl_12': 8.0,
     'tbl_13': 8.0,
     'tbl_14': 8.0,
     'tbl_15': 8.0,
     'tbl_16': 8.0,
     'tbl_17': 8.0,
     'tbl_18': 8.0,
     'tbl_19': 8.0,
     'tbl_20': 8.0,
     'tbl_21': 8.0,
     'tbl_22': 8.0,
     'tbl_23': 8.0,
     'tbl_24': 8.0,
     'tbl_25': 8.0,
     'tbl_26': 8.0,
     'tbl_27': 8.0,
     'tbl_28': 8.0,
     'tbl_29': 8.0,
     'tbl_30': 8.0,
     'tbl_31': 8.0,
     'L0_rec_W0': 3.521,
     'L0_rec_W1': 8.0,
     'L0_rec_W2': 8.0,
     'dense_ctx': 7.165}
    for name, (base, spread) in spreads.items():
        noise = np.random.default_rng([zlib.crc32(name.encode()), seed]).standard_normal(out[name].shape)
        drawn = base * np.exp(spread * noise) if base else spread * noise
        out[name] = jnp.asarray(drawn.astype(out[name].dtype))
    for name, factor in factors.items():
        out[name] = (out[name] * factor).astype(out[name].dtype)
    return out
```

```python
from contextlib import ExitStack

import concourse.bass as bass
from concourse import mybir

F32 = mybir.dt.float32
BF16 = mybir.dt.bfloat16
I32 = mybir.dt.int32
ALU = mybir.AluOpType
ACT = mybir.ActivationFunctionType
AXX = mybir.AxisListType.X

P = 128
BATCH, FIELDS, DIM, UNITS = 1024, 32, 16, 64
QUADS = 4
PAIRS = 16
JS = BATCH // PAIRS // QUADS
GCOLS = JS * DIM
COLS = QUADS * GCOLS
HALF = COLS // 2
ROWS = HALF // DIM
SUMS = 5
SQ = 2 * SUMS
TS, SS = FIELDS // 4, UNITS // 32
RING = 4
BANKS = 4
GATHERED = 16 * JS
REPLICATED = 16 * 4
STACKED = 16 * QUADS
LOOPS = (PAIRS - 2) // 2
MLP1, MLP2 = 512, 256


def cin_tower(nc, ids, base, table, pick, w0_ab, w0, w1, w2, dense, wt1, bt1, wt2, bt2, wt3, out):
    ctx = ExitStack()
    with ctx:
        def sb(name, shape, dt=F32):
            return ctx.enter_context(nc.sbuf_tensor(name, shape, dt))

        def sem(name):
            return ctx.enter_context(nc.semaphore(name))

        ids_sb = sb("ids_sb", [P, BATCH // QUADS], I32)
        base_sb = sb("base_sb", [P, 1], I32)
        rows_sb = sb("rows_sb", [P, BATCH // QUADS], I32)
        emb = [sb(f"emb{b}", [P, GCOLS]) for b in range(2)]
        rest = sb("rest", [P, GCOLS])
        split = sb("split", [P, 3, GCOLS], BF16)
        stack = [sb(f"stack{b}", [3 * FIELDS, COLS], BF16) for b in range(2)]
        xrep = [sb(f"xrep{b}", [P, TS, COLS]) for b in range(2)]
        x_dram = nc.dram_tensor("x_scratch", (2, FIELDS, COLS), F32, kind="Internal").ap()
        pick_sb = sb("pick_sb", [3 * FIELDS, SUMS * P], BF16)
        w0_sb = sb("w0_sb", [P, SUMS, UNITS])
        w1_sb = sb("w1_sb", [P, TS, SS, UNITS])
        w2_sb = sb("w2_sb", [P, TS, SS, UNITS])
        squares = sb("squares", [P, SUMS, COLS])
        prod = [sb(f"prod{r}", [P, SS, COLS]) for r in range(RING)]
        y = [sb(f"y{n}", [P, HALF]) for n in range(3)]
        yrep1 = sb("yrep1", [P, SS, COLS])
        yrep2 = [sb(f"yrep2_{b}", [P, SS, COLS]) for b in range(2)]
        zt = sb("zt", [P, 3, PAIRS * ROWS])
        pick_f = prod[0][0:3 * FIELDS, 0, 0:SUMS * P]
        w0_a = prod[1][:, 0, 0:4 * UNITS]
        w0_b = prod[1][:, 0, 4 * UNITS:8 * UNITS]
        w0_diag = prod[1][0:FIELDS, 1, 0:UNITS]
        w0_rsum = prod[1][0:FIELDS, 1, UNITS:2 * UNITS]
        w0_csum = prod[1][0:FIELDS, 1, 2 * UNITS:3 * UNITS]
        w0_rows = prod[2][0:FIELDS, :, :].rearrange("m s n -> m (s n)")
        w0_cols = prod[3][0:FIELDS, :, :].rearrange("m s n -> m (s n)")
        wt1_sb = sb("wt1_sb", [P, 3, MLP1])
        wtd_sb = sb("wtd_sb", [DIM, MLP1])
        wt2_sb = sb("wt2_sb", [P, MLP1 // P, MLP2])
        wt3_sb = sb("wt3_sb", [P, MLP2 // P])
        bt1_sb = sb("bt1_sb", [P, MLP1 // P])
        bt2_sb = sb("bt2_sb", [P, MLP2 // P])
        dense_sb = sb("dense_sb", [DIM, 2, PAIRS * ROWS])
        h1 = xrep[0][:, 0:4, :].rearrange("p k (c n) -> p k c n", c=2)
        h2 = xrep[1][:, 0:2, :].rearrange("p k (c n) -> p k c n", c=2)
        score = yrep1[0:1, 0, :]

        acc = [ctx.enter_context(nc.psum_tensor(f"acc{n}", [P, HALF], F32)) for n in range(3)]
        sums = [ctx.enter_context(nc.psum_tensor(f"sums{n}", [P, HALF], F32)) for n in range(BANKS)]

        ids_in = sem("ids_in")
        rows_ready = sem("rows_ready")
        gathered = [sem(f"gathered{b}") for b in range(2)]
        split_step = sem("split_step")
        stack_in = [sem(f"stack_in{b}") for b in range(2)]
        x_stored = [sem(f"x_stored{b}") for b in range(2)]
        xrep_in = [[sem(f"xrep_in{b}_{t}") for t in range(TS)] for b in range(2)]
        pick_in = sem("pick_in")
        pick_ready = sem("pick_ready")
        w0_in = sem("w0_in")
        w0_step = sem("w0_step")
        w12_in = sem("w12_in")
        mlp_in = sem("mlp_in")
        sums_ready = sem("sums_ready")
        squared = sem("squared")
        layer0_done = sem("layer0_done")
        relued = [sem(f"relued{n}") for n in range(3)]
        reduced = [sem(f"reduced{n}") for n in range(3)]
        yrep1_in = sem("yrep1_in")
        yrep2_in = [sem(f"yrep2_in{b}") for b in range(2)]
        prod_ready = sem("prod_ready")
        prod_used = sem("prod_used")
        h1_done = sem("h1_done")
        h1_ready = sem("h1_ready")
        h2_done = sem("h2_done")
        h2_ready = sem("h2_ready")
        y_done = sem("y_done")
        y_ready = sem("y_ready")
        out_stored = sem("out_stored")

        def uses(half, par, ahead):
            return half + (par + ahead) // 2 + 1

        block = ctx.enter_context(nc.Block())

        @block.gpsimd
        def _(pool):
            pool.wait_ge(ids_in, 32)
            nc.gpsimd.tensor_tensor(rows_sb[:], ids_sb[:], base_sb[:].to_broadcast([P, BATCH // QUADS]),
                                    ALU.add).then_inc(rows_ready, 1)
            pool.wait_ge(rows_ready, 1)
            for p in range(PAIRS):
                par = p % 2
                if p >= 2:
                    pool.wait_ge(x_stored[par], 16 * (p // 2))
                    pool.wait_ge(split_step, 4 * (p - 1))
                for j in range(JS):
                    nc.gpsimd.indirect_dma_start(
                        emb[par][:, j * DIM:j * DIM + DIM], None, table,
                        bass.IndirectOffsetOnAxis(ap=rows_sb[:, JS * p + j:JS * p + j + 1], axis=0),
                    ).then_inc(gathered[par], 16)
                now = emb[par][:]
                pool.wait_ge(gathered[par], GATHERED * (p // 2 + 1))
                if p >= 1:
                    pool.wait_ge(stack_in[1 - par], STACKED * ((p + 1) // 2))
                nc.gpsimd.tensor_copy(split[:, 0, :], now).then_inc(split_step, 1)
                pool.wait_ge(split_step, 4 * p + 1)
                nc.gpsimd.tensor_tensor(rest[:], now, split[:, 0, :], ALU.subtract).then_inc(split_step, 1)
                pool.wait_ge(split_step, 4 * p + 2)
                nc.gpsimd.tensor_copy(split[:, 1, :], rest[:]).then_inc(split_step, 1)
                pool.wait_ge(split_step, 4 * p + 3)
                nc.gpsimd.tensor_tensor(split[:, 2, :], rest[:], split[:, 1, :], ALU.subtract).then_inc(split_step, 1)

        @block.sync
        def _(sp):
            def store_x(p, par, half):
                sp.wait_ge(gathered[par], GATHERED * (half + 1))
                sp.dma_start(x_dram[par].rearrange("m (q x) -> q m x", q=QUADS), emb[par][:]
                             ).then_inc(x_stored[par], 16)

            def load_stack(p, par, half):
                sp.wait_ge(split_step, 4 * p + 4)
                for q in range(QUADS):
                    sp.dma_start(stack[par][:, GCOLS * q:GCOLS * q + GCOLS],
                                 split[FIELDS * q:FIELDS * q + FIELDS, :, :]).then_inc(stack_in[par], 16)

            def load_xrep(p, par, half, before):
                sp.wait_ge(x_stored[par], 16 * (half + 1))
                sp.nop(nofuse=True)
                for t in range(TS):
                    if before is not None:
                        sp.wait_ge(prod_ready, before + t + 1)
                    src = x_dram[par:par + 1, 4 * t:4 * t + 4, :].to_broadcast([32, 4, COLS])
                    sp.dma_start(xrep[par][:, t, :], src).then_inc(xrep_in[par][t], 16)

            sp.dma_start(ids_sb[:], ids).then_inc(ids_in, 16)
            sp.dma_start(base_sb[:], base).then_inc(ids_in, 16)
            sp.dma_start(w0_a, w0_ab[:, 0, :]).then_inc(w0_in, 16)
            sp.dma_start(w0_b, w0_ab[:, 1, :]).then_inc(w0_in, 16)
            sp.dma_start(w0_diag, bass.AP(w0.tensor, w0.offset, [[(FIELDS + 1) * UNITS, FIELDS], [1, UNITS]])
                         ).then_inc(w0_in, 16)
            sp.dma_start(w0_rows, w0.rearrange("m h k -> m (h k)")).then_inc(w0_in, 16)
            sp.dma_start(w0_cols.rearrange("h (m k) -> h m k", k=UNITS), w0.rearrange("m h k -> h m k")
                         ).then_inc(w0_in, 16)
            store_x(0, 0, 0)
            load_stack(0, 0, 0)
            load_xrep(0, 0, 0, None)
            store_x(1, 1, 0)
            load_stack(1, 1, 0)
            load_xrep(1, 1, 0, None)
            sp.wait_ge(prod_ready, TS)
            store_x(2, 0, 1)
            load_stack(2, 0, 1)
            with sp.Fori(0, LOOPS - 1) as i:
                for par in (1, 0):
                    p = 2 * i + 2 - par
                    half = i + 1 - par
                    load_xrep(p + 1, 1 - par, half + par, 16 * p)
                    store_x(p + 2, par, half + 1)
                    load_stack(p + 2, par, half + 1)
            p = PAIRS - 3
            load_xrep(p + 1, 0, p // 2 + 1, 16 * p)
            store_x(p + 2, 1, p // 2 + 1)
            load_stack(p + 2, 1, p // 2 + 1)
            p = PAIRS - 2
            load_xrep(p + 1, 1, p // 2, 16 * p)
            sp.wait_ge(y_ready, 1)
            sp.dma_start(out, score).then_inc(out_stored, 16)
            sp.wait_ge(out_stored, 16)

        @block.scalar
        def _(act):
            def replicate(dst, src, arrived):
                pitch = src.ap[0][0]
                for s in range(SS):
                    for c in range(2):
                        act.dma_start(dst[:, s, HALF * c:HALF * c + HALF],
                                      bass.AP(src.tensor, src.offset + (UNITS * c + 32 * s) * pitch,
                                              [[pitch, 32], [0, 4], [1, HALF]])).then_inc(arrived, 16)

            def squares_of(p, par):
                if not (isinstance(p, int) and p < 1):
                    act.wait_ge(layer0_done, p)
                for i in range(SQ):
                    k, c = i // 2, i % 2
                    n = P if k < SUMS - 1 else FIELDS
                    act.wait_ge(sums_ready, SQ * p + i + 1)
                    nc.scalar.activation(squares[0:n, k, HALF * c:HALF * c + HALF],
                                         sums[(SQ * par + i) % BANKS][0:n, :], ACT.Square).then_inc(squared, 1)

            def relu0(p):
                act.wait_ge(layer0_done, p + 1)
                if not (isinstance(p, int) and p < 1):
                    act.wait_ge(reduced[0], p)
                    act.wait_ge(yrep1_in, REPLICATED * p)
                nc.scalar.activation(y[0][:], acc[0][:], ACT.Relu).then_inc(relued[0], 1)
                act.wait_ge(relued[0], p + 1)
                if not (isinstance(p, int) and p < 1):
                    act.wait_ge(prod_ready, 16 * (p - 1) if not (isinstance(p, int) and p == 1) else TS)
                replicate(yrep1, y[0][:], yrep1_in)

            def relu1(p, par, half):
                act.wait_ge(prod_used, 16 * p if not (isinstance(p, int) and p < 1) else TS)
                if not (isinstance(p, int) and p < 1):
                    act.wait_ge(reduced[1], p)
                    act.wait_ge(yrep2_in[1 - par], REPLICATED * uses(half, par, -1))
                nc.scalar.activation(y[1][:], acc[1][:], ACT.Relu).then_inc(relued[1], 1)
                act.wait_ge(relued[1], p + 1)
                if not (isinstance(p, int) and p < 2):
                    act.wait_ge(prod_ready, 16 * p - 8)
                replicate(yrep2[par], y[1][:], yrep2_in[par])

            def relu2(p, used):
                act.wait_ge(prod_used, used)
                if not (isinstance(p, int) and p < 1):
                    act.wait_ge(reduced[2], p)
                nc.scalar.activation(y[2][:], acc[2][:], ACT.Relu).then_inc(relued[2], 1)

            act.dma_start(pick_f, pick).then_inc(pick_in, 16)
            act.dma_start(w1_sb[:].rearrange("p t s k -> p (t s k)"), w1).then_inc(w12_in, 16)
            act.dma_start(w2_sb[:].rearrange("p t s k -> p (t s k)"), w2).then_inc(w12_in, 16)
            for c in range(2):
                act.dma_start(wt1_sb[UNITS * c:UNITS * c + UNITS],
                              wt1[0:3 * UNITS].rearrange("(l k) n -> k l n", k=UNITS)).then_inc(mlp_in, 16)
            act.dma_start(wtd_sb[:], wt1[3 * UNITS:3 * UNITS + DIM]).then_inc(mlp_in, 16)
            act.dma_start(wt2_sb[:], wt2.rearrange("(t p) n -> p t n", p=P)).then_inc(mlp_in, 16)
            act.dma_start(wt3_sb[:], wt3).then_inc(mlp_in, 16)
            act.dma_start(bt1_sb[:], bt1).then_inc(mlp_in, 16)
            act.dma_start(bt2_sb[:], bt2).then_inc(mlp_in, 16)
            act.dma_start(dense_sb[:].rearrange("f c n -> f (c n)"), dense).then_inc(mlp_in, 16)
            squares_of(0, 0)
            relu0(0)
            squares_of(1, 1)
            relu1(0, 0, 0)
            relu0(1)
            with act.Fori(0, LOOPS) as i:
                for par in (1, 0):
                    p = 2 * i + 2 - par
                    half = i + 1 - par
                    squares_of(p + 1, 1 - par)
                    relu1(p, par, half)
                    relu0(p + 1)
                    relu2(p - 1, 16 * p + 8)
            last = PAIRS - 1
            relu1(last, 1, last // 2)
            relu2(last - 1, 16 * last + 8)
            relu2(last, 16 * last + 16)
            act.wait_ge(mlp_in, 16 * 8)
            for m in range(MLP1 // P):
                for c in range(2):
                    act.wait_ge(h1_done, 2 * m + c + 1)
                    nc.scalar.activation(h1[:, m, c, :], (acc + sums)[(2 * m + c) % 6][:], ACT.Relu,
                                         bias=bt1_sb[:, m:m + 1]).then_inc(h1_ready, 1)
            for m in range(MLP2 // P):
                for c in range(2):
                    act.wait_ge(h2_done, 2 * m + c + 1)
                    nc.scalar.activation(h2[:, m, c, :], (acc + sums)[(2 + 2 * m + c) % 6][:], ACT.Relu,
                                         bias=bt2_sb[:, m:m + 1]).then_inc(h2_ready, 1)
            act.wait_ge(y_done, 1)
            for c in range(2):
                last_copy = nc.scalar.copy(score[:, HALF * c:HALF * c + HALF], acc[c][0:1, :])
            last_copy.then_inc(y_ready, 1)

        @block.vector
        def _(dve):
            def products(at, t, xr, yr):
                if not (isinstance(at, int) and at < RING):
                    dve.wait_ge(prod_used, at - RING + 1)
                nc.vector.tensor_tensor(prod[t % RING][:], xr[:, t:t + 1, :].to_broadcast([P, SS, COLS]), yr[:],
                                        ALU.mult).then_inc(prod_ready, 1)

            def reduce_d(n, p):
                dve.wait_ge(relued[n], p + 1)
                nc.vector.tensor_reduce(zt[:, n, bass.ds(p * ROWS, ROWS)],
                                        y[n][:].rearrange("p (r d) -> p r d", d=DIM), AXX,
                                        ALU.add).then_inc(reduced[n], 1)

            def layer1(p, par, half, at, y2=True):
                dve.wait_ge(yrep1_in, REPLICATED * (p + 1))
                for t in range(TS):
                    dve.wait_ge(xrep_in[par][t], 16 * (half + 1))
                    products(at + t, t, xrep[par], yrep1)
                    if t == 2 and y2:
                        reduce_d(2, p - 2)

            def layer2(p, par, half, at, y1, y0):
                dve.wait_ge(yrep2_in[par], REPLICATED * (half + 1))
                for t in range(TS):
                    products(at + t, t, xrep[par], yrep2[par])
                    if t == 1 and y1 is not None:
                        reduce_d(1, y1)
                    if t == 5 and y0 is not None:
                        reduce_d(0, y0)

            dve.wait_ge(pick_in, 16)
            nc.vector.tensor_copy(pick_sb[:], pick_f).then_inc(pick_ready, 1)
            dve.wait_ge(w0_in, 16 * 5)
            pairs_w = w0_sb[:, 0:4, :].rearrange("p u k -> p (u k)")
            diag_w = w0_sb[0:FIELDS, 4, :]
            nc.vector.tensor_tensor(w0_a, w0_a, w0_b, ALU.add).then_inc(w0_step, 1)
            nc.vector.tensor_reduce(w0_rsum, w0_rows.rearrange("m (h k) -> m k h", k=UNITS), AXX,
                                    ALU.add).then_inc(w0_step, 1)
            nc.vector.tensor_reduce(w0_csum, w0_cols.rearrange("h (m k) -> h k m", k=UNITS), AXX,
                                    ALU.add).then_inc(w0_step, 1)
            dve.wait_ge(w0_step, 3)
            nc.vector.tensor_scalar_mul(pairs_w, w0_a, 0.5).then_inc(w0_step, 1)
            nc.vector.tensor_tensor(w0_rsum, w0_rsum, w0_csum, ALU.add).then_inc(w0_step, 1)
            dve.wait_ge(w0_step, 5)
            nc.vector.tensor_scalar_mul(w0_sb[96:128, 3, :], w0_sb[96:128, 3, :], 0.5).then_inc(w0_step, 1)
            nc.vector.tensor_scalar_mul(w0_rsum, w0_rsum, -0.5).then_inc(w0_step, 1)
            dve.wait_ge(w0_step, 7)
            nc.vector.scalar_tensor_tensor(out=diag_w, in0=w0_diag, scalar=2.0, in1=w0_rsum, op0=ALU.mult,
                                           op1=ALU.add).then_inc(w0_step, 1)
            dve.wait_ge(w0_step, 8)
            reduce_d(0, 0)
            layer1(0, 0, 0, 0, y2=False)
            reduce_d(1, 0)
            reduce_d(0, 1)
            layer1(1, 1, 0, TS, y2=False)
            layer2(0, 0, 0, 2 * TS, 1, 2)
            layer1(2, 0, 1, 3 * TS)
            layer2(1, 1, 0, 4 * TS, 2, 3)
            with dve.Fori(1, LOOPS) as i:
                for par in (1, 0):
                    p = 2 * i + 2 - par
                    half = i + 1 - par
                    layer1(p, par, half, 16 * p - 8)
                    layer2(p - 1, 1 - par, half + par - 1, 16 * p, p, p + 1)
            last = PAIRS - 1
            layer1(last, 1, last // 2, 16 * last - 8)
            layer2(last - 1, 0, last // 2, 16 * last, last, None)
            dve.wait_ge(yrep2_in[1], REPLICATED * (last // 2 + 1))
            for t in range(TS):
                products(16 * last + 8 + t, t, xrep[1], yrep2[1])
                if t == 2:
                    reduce_d(2, last - 1)
            reduce_d(2, last)

        @block.tensor
        def _(pe):
            def pair_sums(p, par, k):
                for c in range(2):
                    i = 2 * k + c
                    if not (isinstance(p, int) and SQ * p + i < BANKS):
                        pe.wait_ge(squared, SQ * p + i - BANKS + 1)
                    n = P if k < SUMS - 1 else FIELDS
                    nc.tensor.matmul(sums[(SQ * par + i) % BANKS][0:n, :], pick_sb[:, P * k:P * k + n],
                                     stack[par][:, HALF * c:HALF * c + HALF], start=True,
                                     stop=True).then_inc(sums_ready, 1)

            def layer0(p, k):
                if k == 0 and not (isinstance(p, int) and p < 1):
                    pe.wait_ge(relued[0], p)
                pe.wait_ge(squared, SQ * p + 2 * k + 2)
                n = P if k < SUMS - 1 else FIELDS
                for c in range(2):
                    mm = nc.tensor.matmul(acc[0][UNITS * c:UNITS * c + UNITS, :], w0_sb[0:n, k, :],
                                          squares[0:n, k, HALF * c:HALF * c + HALF], start=(k == 0),
                                          stop=(k == SUMS - 1))
                if k == SUMS - 1:
                    mm.then_inc(layer0_done, 1)

            def contract(at, t, w, to):
                pe.wait_ge(prod_ready, at + t + 1)
                for s in range(SS):
                    for c in range(2):
                        mm = nc.tensor.matmul(to[UNITS * c:UNITS * c + UNITS, :], w[:, t, s, :],
                                              prod[t % RING][:, s, HALF * c:HALF * c + HALF],
                                              start=(t == 0 and s == 0), stop=(t == TS - 1 and s == SS - 1))
                    if s == SS - 1:
                        mm.then_inc(prod_used, 1)

            def layer1(p, at, par_next):
                if not (isinstance(p, int) and p < 1):
                    pe.wait_ge(relued[1], p)
                for t in range(TS):
                    contract(at, t, w1_sb, acc[1])
                    if t == 0 and par_next is not None:
                        pe.wait_ge(stack_in[par_next[0]], STACKED * par_next[1])
                    if t < SUMS and par_next is not None:
                        pair_sums(p + 1, par_next[0], t)

            def layer2(p, at, next_pair):
                if not (isinstance(p, int) and p < 1):
                    pe.wait_ge(relued[2], p)
                for t in range(TS):
                    contract(at, t, w2_sb, acc[2])
                    if next_pair is not None:
                        for k in ((0, 1), (2, 3), (4,))[t] if t < 3 else ():
                            layer0(next_pair, k)

            pe.wait_ge(pick_ready, 1)
            pe.wait_ge(stack_in[0], STACKED)
            pe.wait_ge(w0_step, 8)
            for k in range(SUMS):
                pair_sums(0, 0, k)
                if k:
                    layer0(0, k - 1)
            layer0(0, SUMS - 1)
            pe.wait_ge(w12_in, 32)
            layer1(0, 0, (1, 1))
            for k in range(SUMS):
                layer0(1, k)
            layer1(1, TS, (0, 2))
            layer2(0, 2 * TS, 2)
            layer1(2, 3 * TS, (1, 2))
            layer2(1, 4 * TS, 3)
            with pe.Fori(1, LOOPS) as i:
                for par in (1, 0):
                    p = 2 * i + 2 - par
                    half = i + 1 - par
                    layer1(p, 16 * p - 8, (1 - par, uses(half, par, 1)))
                    layer2(p - 1, 16 * p, p + 1)
            last = PAIRS - 1
            layer1(last, 16 * last - 8, None)
            layer2(last - 1, 16 * last, None)
            layer2(last, 16 * last + 8, None)

            banks = acc + sums
            pe.wait_ge(mlp_in, 16 * 8)
            pe.wait_ge(relued[2], PAIRS)
            for n in range(3):
                pe.wait_ge(reduced[n], PAIRS)
            for m in range(MLP1 // P):
                for n in range(4):
                    for c in range(2):
                        i = 2 * m + c
                        if n == 0 and i >= 6:
                            pe.wait_ge(h1_ready, i - 5)
                        lhs = wt1_sb[UNITS * c:UNITS * c + UNITS, n] if n < 3 else wtd_sb[:]
                        rhs = zt[UNITS * c:UNITS * c + UNITS, n, :] if n < 3 else dense_sb[:, c, :]
                        mm = nc.tensor.matmul(banks[i % 6][:], lhs[:, P * m:P * m + P], rhs, start=(n == 0),
                                              stop=(n == 3))
                        if n == 3:
                            mm.then_inc(h1_done, 1)
            for m in range(MLP2 // P):
                for c in range(2):
                    i = 2 * m + c
                    pe.wait_ge(h1_ready, 7 + c)
                    for k in range(MLP1 // P):
                        mm = nc.tensor.matmul(banks[(2 + i) % 6][:], wt2_sb[:, k, P * m:P * m + P], h1[:, k, c, :],
                                              start=(k == 0), stop=(k == MLP1 // P - 1))
                    mm.then_inc(h2_done, 1)
            pe.wait_ge(h2_ready, 4)
            for c in range(2):
                for k in range(MLP2 // P):
                    mm = nc.tensor.matmul(acc[c][0:1, :], wt3_sb[:, k:k + 1], h2[:, k, c, :], start=(k == 0),
                                          stop=(k == MLP2 // P - 1))
            mm.then_inc(y_done, 1)


def kernel(**inputs):
    import numpy as np
    import concourse.bacc as bacc
    from concourse.bass_utils import run_bass_kernel_spmd

    x = {k: np.asarray(v) for k, v in inputs.items()}
    tables = [x[f"tbl_{f}"] for f in range(FIELDS)]
    starts = np.cumsum([0] + [t.shape[0] for t in tables[:-1]]).astype(np.int32)
    pick = np.zeros((FIELDS, 3, SUMS, P), np.float32)
    m = np.arange(FIELDS)
    first, second = [], []
    for u in range(4):
        for i in range(4):
            h = (m + 4 * u + i + 1) % FIELDS
            pick[m, :, u, FIELDS * i + m] = 1.0
            pick[h, :, u, FIELDS * i + m] = 1.0
            first.append(m)
            second.append(h)
    pick[m, :, 4, m] = 1.0
    first, second = np.concatenate(first), np.concatenate(second)
    w0 = x["L0_rec_W0"]
    w0_ab = np.stack([w0[first, second], w0[second, first]]).reshape(2, 4, P, UNITS).transpose(2, 0, 1, 3)

    def product_weights(w):
        return w.reshape(TS, 4, SS, 32, UNITS).transpose(3, 1, 0, 2, 4).reshape(P, TS * SS * UNITS)

    arrays = {
        "ids": x["ids"].reshape(BATCH // QUADS, P).T,
        "base": np.tile(starts, QUADS).reshape(P, 1),
        "table": np.concatenate(tables, axis=0),
        "pick": pick.reshape(3 * FIELDS, SUMS * P),
        "w0_ab": w0_ab.reshape(P, 2, 4 * UNITS),
        "w0": w0,
        "w1": product_weights(x["L0_rec_W1"]),
        "w2": product_weights(x["L0_rec_W2"]),
        "dense": x["dense_ctx"].reshape(PAIRS, JS, 2, 2, DIM).transpose(4, 2, 0, 3, 1).reshape(DIM, BATCH),
        "wt1": x["W_top1"],
        "bt1": x["b_top1"].reshape(MLP1 // P, P).T,
        "wt2": x["W_top2"],
        "bt2": x["b_top2"].reshape(MLP2 // P, P).T,
        "wt3": x["W_top3"].reshape(MLP2 // P, P).T,
    }
    arrays = {k: np.ascontiguousarray(v) for k, v in arrays.items()}
    nc = bacc.Bacc("TRN2", target_bir_lowering=False, num_devices=1)
    args = [nc.dram_tensor(f"in_{k}", v.shape, mybir.dt.from_np(v.dtype), kind="ExternalInput").ap()
            for k, v in arrays.items()]
    out = nc.dram_tensor("out_score", (1, BATCH), F32, kind="ExternalOutput").ap()
    cin_tower(nc, *args, out)
    got = run_bass_kernel_spmd(nc, [{f"in_{k}": v for k, v in arrays.items()}], core_ids=[0]).results[0]["out_score"]
    return got.reshape(2, PAIRS, 2, JS).transpose(1, 3, 0, 2).reshape(BATCH, 1)
```

```python
from contextlib import ExitStack

import concourse.bass as bass
from concourse import mybir

F32 = mybir.dt.float32
BF16 = mybir.dt.bfloat16
I32 = mybir.dt.int32
ALU = mybir.AluOpType
ACT = mybir.ActivationFunctionType
AXX = mybir.AxisListType.X

P = 128
BATCH, FIELDS, DIM, UNITS = 1024, 32, 16, 64
QUADS = 4
PAIRS = 16
JS = BATCH // PAIRS // QUADS
GCOLS = JS * DIM
COLS = QUADS * GCOLS
HALF = COLS // 2
ROWS = HALF // DIM
SUMS = 5
SQ = 2 * SUMS
TS, SS = FIELDS // 4, UNITS // 32
RING = 4
BANKS = 2
GATHERED = 16 * JS
REPLICATED = 16 * 4
STACKED = 16 * QUADS
LOOPS = (PAIRS - 2) // 2
MLP1, MLP2 = 512, 256
GROUP = 2 * BATCH // PAIRS


def cin_tower(nc, ids, base, table, pick, w0_ab, w0, w1, w2, dense, wt1, bt1, wt2, bt2, wt3, out):
    ctx = ExitStack()
    with ctx:
        def sb(name, shape, dt=F32):
            return ctx.enter_context(nc.sbuf_tensor(name, shape, dt))

        def sem(name):
            return ctx.enter_context(nc.semaphore(name))

        ids_sb = sb("ids_sb", [P, BATCH // QUADS], I32)
        base_sb = sb("base_sb", [P, 1], I32)
        rows_sb = sb("rows_sb", [P, BATCH // QUADS], I32)
        emb = [sb(f"emb{b}", [P, 3, GCOLS]) for b in range(2)]
        stack = [sb(f"stack{b}", [3 * FIELDS, COLS]) for b in range(2)]
        xrep = [sb(f"xrep{b}", [P, TS, COLS]) for b in range(2)]
        x_dram = nc.dram_tensor("x_scratch", (2, FIELDS, COLS), F32, kind="Internal").ap()
        pick_sb = sb("pick_sb", [3 * FIELDS, SUMS * P], BF16)
        w0_sb = sb("w0_sb", [P, SUMS, UNITS])
        w1_sb = sb("w1_sb", [P, TS, SS, UNITS])
        w2_sb = sb("w2_sb", [P, TS, SS, UNITS])
        squares = sb("squares", [P, SUMS, COLS])
        prod = [sb(f"prod{r}", [P, SS, COLS]) for r in range(RING)]
        y = [sb(f"y{n}", [P, HALF]) for n in range(3)]
        yrep1 = sb("yrep1", [P, SS, COLS])
        yrep2 = [sb(f"yrep2_{b}", [P, SS, COLS]) for b in range(2)]
        zt = sb("zt", [P, 3, PAIRS, ROWS])
        pick_f = prod[0][0:3 * FIELDS, 0, 0:SUMS * P]
        w0_a = prod[1][:, 0, 0:4 * UNITS]
        w0_b = prod[1][:, 0, 4 * UNITS:8 * UNITS]
        w0_diag = prod[1][0:FIELDS, 1, 0:UNITS]
        w0_rsum = prod[1][0:FIELDS, 1, UNITS:2 * UNITS]
        w0_csum = prod[1][0:FIELDS, 1, 2 * UNITS:3 * UNITS]
        w0_rows = prod[2][0:FIELDS, :, :].rearrange("m s n -> m (s n)")
        w0_cols = prod[3][0:FIELDS, :, :].rearrange("m s n -> m (s n)")
        wt1_sb = sb("wt1_sb", [P, 2, MLP1])
        wt2_sb = sb("wt2_sb", [P, MLP1 // P, MLP2])
        wt3_sb = sb("wt3_sb", [P, MLP2 // P])
        bt1_sb = sb("bt1_sb", [P, MLP1 // P])
        bt2_sb = sb("bt2_sb", [P, MLP2 // P])
        feat = sb("feat", [P, 2, GROUP])
        h1 = sb("h1", [P, MLP1 // P, GROUP])
        h2 = sb("h2", [P, MLP2 // P, GROUP])
        score = sb("score", [1, BATCH])

        acc = [ctx.enter_context(nc.psum_tensor(f"acc{n}", [P, HALF], F32)) for n in range(3)]
        sums = [ctx.enter_context(nc.psum_tensor(f"sums{n}", [P, HALF], F32)) for n in range(BANKS)]

        h1_acc = ctx.enter_context(nc.psum_tensor("h1_acc", [P, MLP1 // P, GROUP], F32))
        h2_acc = ctx.enter_context(nc.psum_tensor("h2_acc", [P, 4, GROUP], F32))
        score_acc = ctx.enter_context(nc.psum_tensor("score_acc", [P, 4, GROUP], F32))

        ids_in = sem("ids_in")
        rows_ready = sem("rows_ready")
        gathered = [sem(f"gathered{b}") for b in range(2)]
        split_first = sem("split_first")
        split_step = sem("split_step")
        stack_in = [sem(f"stack_in{b}") for b in range(2)]
        x_stored = [sem(f"x_stored{b}") for b in range(2)]
        xrep_in = [[sem(f"xrep_in{b}_{t}") for t in range(TS)] for b in range(2)]
        pick_in = sem("pick_in")
        pick_ready = sem("pick_ready")
        w0_in = sem("w0_in")
        w0_step = sem("w0_step")
        w12_in = sem("w12_in")
        mlp_in = sem("mlp_in")
        sums_ready = sem("sums_ready")
        squared = sem("squared")
        layer0_done = sem("layer0_done")
        relued = [sem(f"relued{n}") for n in range(3)]
        reduced = [sem(f"reduced{n}") for n in range(3)]
        yrep1_in = sem("yrep1_in")
        yrep2_in = [sem(f"yrep2_in{b}") for b in range(2)]
        prod_ready = sem("prod_ready")
        prod_used = sem("prod_used")
        feat_in = sem("feat_in")
        h1_done = sem("h1_done")
        h1_ready = sem("h1_ready")
        h2_done = sem("h2_done")
        h2_ready = sem("h2_ready")
        score_done = sem("score_done")
        score_ready = sem("score_ready")
        out_stored = sem("out_stored")

        def uses(half, par, ahead):
            return half + (par + ahead) // 2 + 1

        def upper(x):
            return x.bitcast(BF16)[:, 1::2]

        block = ctx.enter_context(nc.Block())

        @block.gpsimd
        def _(pool):
            pool.wait_ge(ids_in, 32)
            nc.gpsimd.tensor_tensor(rows_sb[:], ids_sb[:], base_sb[:].to_broadcast([P, BATCH // QUADS]),
                                    ALU.add).then_inc(rows_ready, 1)
            pool.wait_ge(rows_ready, 1)
            for p in range(PAIRS):
                par = p % 2
                if p >= 2:
                    pool.wait_ge(x_stored[par], 16 * (p // 2))
                    pool.wait_ge(stack_in[par], STACKED * (p // 2))
                for j in range(JS):
                    nc.gpsimd.indirect_dma_start(
                        emb[par][:, 0, j * DIM:j * DIM + DIM], None, table,
                        bass.IndirectOffsetOnAxis(ap=rows_sb[:, JS * p + j:JS * p + j + 1], axis=0),
                    ).then_inc(gathered[par], 16)
                if p >= 1:
                    pool.wait_ge(gathered[par], GATHERED * (p // 2 + 1))
                    for part in range(2):
                        if part == 1:
                            pool.wait_ge(split_step, 2 * p - 1)
                        nc.gpsimd.tensor_tensor(emb[par][:, part + 1, :], emb[par][:, part, :],
                                                upper(emb[par][:, part, :]), ALU.subtract).then_inc(split_step, 1)

        @block.sync
        def _(sp):
            def store_x(p, par, half):
                sp.wait_ge(gathered[par], GATHERED * (half + 1))
                sp.dma_start(x_dram[par].rearrange("m (q x) -> q m x", q=QUADS), emb[par][:, 0, :]
                             ).then_inc(x_stored[par], 16)

            def load_stack(p, par, half):
                if isinstance(p, int) and p < 1:
                    sp.wait_ge(split_first, 2)
                else:
                    sp.wait_ge(split_step, 2 * p)
                for q in range(QUADS):
                    sp.dma_start(stack[par][:, GCOLS * q:GCOLS * q + GCOLS],
                                 emb[par][FIELDS * q:FIELDS * q + FIELDS, :, :]).then_inc(stack_in[par], 16)

            def load_xrep(p, par, half, before):
                sp.wait_ge(x_stored[par], 16 * (half + 1))
                sp.nop(nofuse=True)
                for t in range(TS):
                    if before is not None:
                        sp.wait_ge(prod_ready, before + t + 1)
                    src = x_dram[par:par + 1, 4 * t:4 * t + 4, :].to_broadcast([32, 4, COLS])
                    sp.dma_start(xrep[par][:, t, :], src).then_inc(xrep_in[par][t], 16)

            def load_z01(g):
                for n in range(2):
                    for c in range(2):
                        sp.dma_start(feat[UNITS * n:UNITS * n + UNITS, 0, :].rearrange(
                            "k (p c r) -> k c p r", p=2, c=2)[:, c],
                            zt[UNITS * c:UNITS * c + UNITS, n, bass.ds(2 * g, 2), :]).then_inc(feat_in, 16)

            def load_z2(g):
                for c in range(2):
                    sp.dma_start(feat[0:UNITS, 1, :].rearrange("k (p c r) -> k c p r", p=2, c=2)[:, c],
                                 zt[UNITS * c:UNITS * c + UNITS, 2, bass.ds(2 * g, 2), :]).then_inc(feat_in, 16)
                sp.dma_start(feat[UNITS:UNITS + DIM, 1, :], dense[:, bass.ds(g * GROUP, GROUP)]).then_inc(feat_in, 16)

            def load_features(g):
                sp.wait_ge(reduced[2], 2 * g + 2)
                sp.nop(nofuse=True)
                if not (isinstance(g, int) and g < 1):
                    sp.wait_ge(h1_done, g)
                    sp.nop(nofuse=True)
                load_z01(g)
                load_z2(g)

            sp.dma_start(ids_sb[:], ids).then_inc(ids_in, 16)
            sp.dma_start(base_sb[:], base).then_inc(ids_in, 16)
            sp.dma_start(w0_a, w0_ab[:, 0, :]).then_inc(w0_in, 16)
            sp.dma_start(w0_b, w0_ab[:, 1, :]).then_inc(w0_in, 16)
            sp.dma_start(w0_diag, bass.AP(w0.tensor, w0.offset, [[(FIELDS + 1) * UNITS, FIELDS], [1, UNITS]])
                         ).then_inc(w0_in, 16)
            sp.dma_start(w0_rows, w0.rearrange("m h k -> m (h k)")).then_inc(w0_in, 16)
            sp.dma_start(w0_cols.rearrange("h (m k) -> h m k", k=UNITS), w0.rearrange("m h k -> h m k")
                         ).then_inc(w0_in, 16)
            store_x(0, 0, 0)
            load_stack(0, 0, 0)
            load_xrep(0, 0, 0, None)
            store_x(1, 1, 0)
            load_stack(1, 1, 0)
            load_xrep(1, 1, 0, None)
            sp.wait_ge(prod_ready, TS)
            store_x(2, 0, 1)
            load_stack(2, 0, 1)
            for p in (1, 2):
                load_xrep(p + 1, 1 - p % 2, (p + 1) // 2, 16 * p)
                store_x(p + 2, p % 2, p // 2 + 1)
                load_stack(p + 2, p % 2, p // 2 + 1)
            with sp.Fori(1, LOOPS - 1) as i:
                for par in (1, 0):
                    p = 2 * i + 2 - par
                    half = i + 1 - par
                    load_xrep(p + 1, 1 - par, half + par, 16 * p)
                    store_x(p + 2, par, half + 1)
                    load_stack(p + 2, par, half + 1)
                    if par == 1:
                        load_features(i - 1)
            p = PAIRS - 3
            load_xrep(p + 1, 0, p // 2 + 1, 16 * p)
            store_x(p + 2, 1, p // 2 + 1)
            load_stack(p + 2, 1, p // 2 + 1)
            load_features(PAIRS // 2 - 3)
            p = PAIRS - 2
            load_xrep(p + 1, 1, p // 2, 16 * p)
            load_features(PAIRS // 2 - 2)
            g = PAIRS // 2 - 1
            sp.wait_ge(reduced[1], PAIRS)
            sp.wait_ge(h1_done, g)
            load_z01(g)
            sp.wait_ge(reduced[2], PAIRS)
            load_z2(g)
            sp.wait_ge(score_ready, PAIRS // 2)
            sp.dma_start(out, score[:]).then_inc(out_stored, 16)
            sp.wait_ge(out_stored, 16)

        @block.scalar
        def _(act):
            def replicate(dst, src, arrived):
                pitch = src.ap[0][0]
                for s in range(SS):
                    for c in range(2):
                        act.dma_start(dst[:, s, HALF * c:HALF * c + HALF],
                                      bass.AP(src.tensor, src.offset + (UNITS * c + 32 * s) * pitch,
                                              [[pitch, 32], [0, 4], [1, HALF]])).then_inc(arrived, 16)

            def squares_of(p, par):
                if not (isinstance(p, int) and p < 1):
                    act.wait_ge(layer0_done, p)
                for i in range(SQ):
                    k, c = i // 2, i % 2
                    n = P if k < SUMS - 1 else FIELDS
                    act.wait_ge(sums_ready, SQ * p + i + 1)
                    nc.scalar.activation(squares[0:n, k, HALF * c:HALF * c + HALF],
                                         sums[(SQ * par + i) % BANKS][0:n, :], ACT.Square).then_inc(squared, 1)

            def relu0(p):
                act.wait_ge(layer0_done, p + 1)
                if not (isinstance(p, int) and p < 1):
                    act.wait_ge(reduced[0], p)
                    act.wait_ge(yrep1_in, REPLICATED * p)
                nc.scalar.activation(y[0][:], acc[0][:], ACT.Relu).then_inc(relued[0], 1)
                act.wait_ge(relued[0], p + 1)
                if not (isinstance(p, int) and p < 1):
                    act.wait_ge(prod_ready, 16 * (p - 1) if not (isinstance(p, int) and p == 1) else TS)
                replicate(yrep1, y[0][:], yrep1_in)

            def relu1(p, par, half):
                act.wait_ge(prod_used, 16 * p if not (isinstance(p, int) and p < 1) else TS)
                if not (isinstance(p, int) and p < 1):
                    act.wait_ge(reduced[1], p)
                    act.wait_ge(yrep2_in[1 - par], REPLICATED * uses(half, par, -1))
                nc.scalar.activation(y[1][:], acc[1][:], ACT.Relu).then_inc(relued[1], 1)
                act.wait_ge(relued[1], p + 1)
                if not (isinstance(p, int) and p < 2):
                    act.wait_ge(prod_ready, 16 * p - 8)
                replicate(yrep2[par], y[1][:], yrep2_in[par])

            def relu2(p, used):
                act.wait_ge(prod_used, used)
                if not (isinstance(p, int) and p < 1):
                    act.wait_ge(reduced[2], p)
                nc.scalar.activation(y[2][:], acc[2][:], ACT.Relu).then_inc(relued[2], 1)

            def rectify_h1(g):
                act.wait_ge(h1_done, g + 1)
                if not (isinstance(g, int) and g < 1):
                    act.wait_ge(h2_done, g)
                for m in range(MLP1 // P):
                    nc.scalar.activation(h1[:, m, :], h1_acc[:, m, :], ACT.Relu,
                                         bias=bt1_sb[:, m:m + 1]).then_inc(h1_ready, 1)

            def rectify_h2(g):
                act.wait_ge(h2_done, g + 1)
                if not (isinstance(g, int) and g < 1):
                    act.wait_ge(score_done, g)
                for m in range(MLP2 // P):
                    nc.scalar.activation(h2[:, m, :], h2_acc[:, m, :], ACT.Relu,
                                         bias=bt2_sb[:, m:m + 1]).then_inc(h2_ready, 1)

            def keep_score(g):
                act.wait_ge(score_done, g + 1)
                nc.scalar.copy(score[:, bass.ds(g * GROUP, GROUP)], score_acc[0:1, 0, :]).then_inc(score_ready, 1)

            act.dma_start(pick_f, pick).then_inc(pick_in, 16)
            act.dma_start(w1_sb[:].rearrange("p t s k -> p (t s k)"), w1).then_inc(w12_in, 16)
            act.dma_start(w2_sb[:].rearrange("p t s k -> p (t s k)"), w2).then_inc(w12_in, 16)
            act.dma_start(wt1_sb[:, 0, :], wt1[0:P]).then_inc(mlp_in, 16)
            act.dma_start(wt1_sb[0:UNITS + DIM, 1, :], wt1[P:P + UNITS + DIM]).then_inc(mlp_in, 16)
            act.dma_start(wt2_sb[:], wt2.rearrange("(t p) n -> p t n", p=P)).then_inc(mlp_in, 16)
            act.dma_start(wt3_sb[:], wt3).then_inc(mlp_in, 16)
            act.dma_start(bt1_sb[:], bt1).then_inc(mlp_in, 16)
            act.dma_start(bt2_sb[:], bt2).then_inc(mlp_in, 16)
            squares_of(0, 0)
            relu0(0)
            squares_of(1, 1)
            relu1(0, 0, 0)
            relu0(1)
            for p in (1, 2):
                squares_of(p + 1, 1 - p % 2)
                relu1(p, p % 2, p // 2)
                relu0(p + 1)
                relu2(p - 1, 16 * p + 8)
            act.wait_ge(mlp_in, 16 * 6)
            with act.Fori(1, LOOPS) as i:
                for par in (1, 0):
                    p = 2 * i + 2 - par
                    half = i + 1 - par
                    squares_of(p + 1, 1 - par)
                    if par == 0:
                        rectify_h1(i - 1)
                    relu1(p, par, half)
                    relu0(p + 1)
                    if par == 0:
                        rectify_h2(i - 1)
                        keep_score(i - 1)
                    relu2(p - 1, 16 * p + 8)
            last = PAIRS - 1
            g = PAIRS // 2 - 2
            relu1(last, 1, last // 2)
            rectify_h1(g)
            rectify_h2(g)
            keep_score(g)
            relu2(last - 1, 16 * last + 8)
            relu2(last, 16 * last + 16)
            rectify_h1(g + 1)
            rectify_h2(g + 1)
            keep_score(g + 1)

        @block.vector
        def _(dve):
            def products(at, t, xr, yr):
                if not (isinstance(at, int) and at < RING):
                    dve.wait_ge(prod_used, at - RING + 1)
                nc.vector.tensor_tensor(prod[t % RING][:], xr[:, t:t + 1, :].to_broadcast([P, SS, COLS]), yr[:],
                                        ALU.mult).then_inc(prod_ready, 1)

            def reduce_d(n, p):
                dve.wait_ge(relued[n], p + 1)
                nc.vector.tensor_reduce(zt[:, n, bass.ds(p, 1), :].rearrange("u o r -> u (o r)"),
                                        y[n][:].rearrange("p (r d) -> p r d", d=DIM), AXX,
                                        ALU.add).then_inc(reduced[n], 1)

            def layer1(p, par, half, at, y2=True):
                dve.wait_ge(yrep1_in, REPLICATED * (p + 1))
                for t in range(TS):
                    dve.wait_ge(xrep_in[par][t], 16 * (half + 1))
                    products(at + t, t, xrep[par], yrep1)
                    if t == 2 and y2:
                        reduce_d(2, p - 2)

            def layer2(p, par, half, at, y1, y0):
                dve.wait_ge(yrep2_in[par], REPLICATED * (half + 1))
                for t in range(TS):
                    products(at + t, t, xrep[par], yrep2[par])
                    if t == 1 and y1 is not None:
                        reduce_d(1, y1)
                    if t == 5 and y0 is not None:
                        reduce_d(0, y0)

            dve.wait_ge(pick_in, 16)
            nc.vector.tensor_copy(pick_sb[:], pick_f).then_inc(pick_ready, 1)
            dve.wait_ge(w0_in, 16 * 5)
            pairs_w = w0_sb[:, 0:4, :].rearrange("p u k -> p (u k)")
            diag_w = w0_sb[0:FIELDS, 4, :]
            nc.vector.tensor_tensor(w0_a, w0_a, w0_b, ALU.add).then_inc(w0_step, 1)
            nc.vector.tensor_reduce(w0_rsum, w0_rows.rearrange("m (h k) -> m k h", k=UNITS), AXX,
                                    ALU.add).then_inc(w0_step, 1)
            nc.vector.tensor_reduce(w0_csum, w0_cols.rearrange("h (m k) -> h k m", k=UNITS), AXX,
                                    ALU.add).then_inc(w0_step, 1)
            dve.wait_ge(w0_step, 3)
            nc.vector.tensor_scalar_mul(pairs_w, w0_a, 0.5).then_inc(w0_step, 1)
            nc.vector.tensor_tensor(w0_rsum, w0_rsum, w0_csum, ALU.add).then_inc(w0_step, 1)
            dve.wait_ge(w0_step, 5)
            nc.vector.tensor_scalar_mul(w0_sb[96:128, 3, :], w0_sb[96:128, 3, :], 0.5).then_inc(w0_step, 1)
            nc.vector.tensor_scalar_mul(w0_rsum, w0_rsum, -0.5).then_inc(w0_step, 1)
            dve.wait_ge(w0_step, 7)
            nc.vector.scalar_tensor_tensor(out=diag_w, in0=w0_diag, scalar=2.0, in1=w0_rsum, op0=ALU.mult,
                                           op1=ALU.add).then_inc(w0_step, 1)
            dve.wait_ge(w0_step, 8)
            for part in range(2):
                if part == 0:
                    dve.wait_ge(gathered[0], GATHERED)
                else:
                    dve.wait_ge(split_first, 1)
                nc.vector.tensor_tensor(emb[0][:, part + 1, :], emb[0][:, part, :], upper(emb[0][:, part, :]),
                                        ALU.subtract).then_inc(split_first, 1)
            reduce_d(0, 0)
            layer1(0, 0, 0, 0, y2=False)
            reduce_d(1, 0)
            reduce_d(0, 1)
            layer1(1, 1, 0, TS, y2=False)
            layer2(0, 0, 0, 2 * TS, 1, 2)
            layer1(2, 0, 1, 3 * TS)
            layer2(1, 1, 0, 4 * TS, 2, 3)
            with dve.Fori(1, LOOPS) as i:
                for par in (1, 0):
                    p = 2 * i + 2 - par
                    half = i + 1 - par
                    layer1(p, par, half, 16 * p - 8)
                    layer2(p - 1, 1 - par, half + par - 1, 16 * p, p, p + 1)
            last = PAIRS - 1
            layer1(last, 1, last // 2, 16 * last - 8)
            layer2(last - 1, 0, last // 2, 16 * last, last, None)
            dve.wait_ge(yrep2_in[1], REPLICATED * (last // 2 + 1))
            for t in range(TS):
                products(16 * last + 8 + t, t, xrep[1], yrep2[1])
                if t == 2:
                    reduce_d(2, last - 1)
            reduce_d(2, last)

        @block.tensor
        def _(pe):
            def pair_sums(p, par, k):
                for c in range(2):
                    i = 2 * k + c
                    if not (isinstance(p, int) and SQ * p + i < BANKS):
                        pe.wait_ge(squared, SQ * p + i - BANKS + 1)
                    n = P if k < SUMS - 1 else FIELDS
                    nc.tensor.matmul(sums[(SQ * par + i) % BANKS][0:n, :], pick_sb[:, P * k:P * k + n],
                                     upper(stack[par][:, HALF * c:HALF * c + HALF]), start=True,
                                     stop=True).then_inc(sums_ready, 1)

            def layer0(p, k):
                if k == 0 and not (isinstance(p, int) and p < 1):
                    pe.wait_ge(relued[0], p)
                pe.wait_ge(squared, SQ * p + 2 * k + 2)
                n = P if k < SUMS - 1 else FIELDS
                for c in range(2):
                    mm = nc.tensor.matmul(acc[0][UNITS * c:UNITS * c + UNITS, :], w0_sb[0:n, k, :],
                                          squares[0:n, k, HALF * c:HALF * c + HALF], start=(k == 0),
                                          stop=(k == SUMS - 1))
                if k == SUMS - 1:
                    mm.then_inc(layer0_done, 1)

            def contract(at, t, w, to):
                pe.wait_ge(prod_ready, at + t + 1)
                for s in range(SS):
                    for c in range(2):
                        mm = nc.tensor.matmul(to[UNITS * c:UNITS * c + UNITS, :], w[:, t, s, :],
                                              prod[t % RING][:, s, HALF * c:HALF * c + HALF],
                                              start=(t == 0 and s == 0), stop=(t == TS - 1 and s == SS - 1))
                    if s == SS - 1:
                        mm.then_inc(prod_used, 1)

            def hidden1(g):
                pe.wait_ge(feat_in, 16 * 7 * (g + 1))
                for m in range(MLP1 // P):
                    for k, n in ((0, P), (1, UNITS + DIM)):
                        mm = nc.tensor.matmul(h1_acc[:, m, :], wt1_sb[0:n, k, P * m:P * m + P], feat[0:n, k, :],
                                              start=(k == 0), stop=(k == 1))
                mm.then_inc(h1_done, 1)

            def hidden2(g):
                pe.wait_ge(h1_ready, MLP1 // P * (g + 1))
                for m in range(MLP2 // P):
                    for k in range(MLP1 // P):
                        mm = nc.tensor.matmul(h2_acc[:, m, :], wt2_sb[:, k, P * m:P * m + P], h1[:, k, :],
                                              start=(k == 0), stop=(k == MLP1 // P - 1))
                mm.then_inc(h2_done, 1)

            def scores(g):
                pe.wait_ge(h2_ready, MLP2 // P * (g + 1))
                if not (isinstance(g, int) and g < 1):
                    pe.wait_ge(score_ready, g)
                for k in range(MLP2 // P):
                    mm = nc.tensor.matmul(score_acc[0:1, 0, :], wt3_sb[:, k:k + 1], h2[:, k, :], start=(k == 0),
                                          stop=(k == MLP2 // P - 1))
                mm.then_inc(score_done, 1)

            def layer1(p, at, par_next, group=None):
                if not (isinstance(p, int) and p < 1):
                    pe.wait_ge(relued[1], p)
                for t in range(TS):
                    contract(at, t, w1_sb, acc[1])
                    if t == 0 and par_next is not None:
                        pe.wait_ge(stack_in[par_next[0]], STACKED * par_next[1])
                    if t < SUMS and par_next is not None:
                        pair_sums(p + 1, par_next[0], t)
                    if t == 5 and group is not None:
                        hidden1(group)

            def layer2(p, at, next_pair, group=None):
                if not (isinstance(p, int) and p < 1):
                    pe.wait_ge(relued[2], p)
                for t in range(TS):
                    contract(at, t, w2_sb, acc[2])
                    if next_pair is not None:
                        for k in ((0, 1), (2, 3), (4,))[t] if t < 3 else ():
                            layer0(next_pair, k)
                    if t == 3 and group is not None:
                        hidden2(group)
                    if t == 5 and group is not None:
                        scores(group)

            pe.wait_ge(pick_ready, 1)
            pe.wait_ge(stack_in[0], STACKED)
            pe.wait_ge(w0_step, 8)
            for k in range(SUMS):
                pair_sums(0, 0, k)
                if k:
                    layer0(0, k - 1)
            layer0(0, SUMS - 1)
            pe.wait_ge(w12_in, 32)
            layer1(0, 0, (1, 1))
            for k in range(SUMS):
                layer0(1, k)
            layer1(1, TS, (0, 2))
            layer2(0, 2 * TS, 2)
            layer1(2, 3 * TS, (1, 2))
            layer2(1, 4 * TS, 3)
            pe.wait_ge(mlp_in, 16 * 6)
            with pe.Fori(1, LOOPS) as i:
                for par in (1, 0):
                    p = 2 * i + 2 - par
                    half = i + 1 - par
                    group = i - 1 if par == 0 else None
                    layer1(p, 16 * p - 8, (1 - par, uses(half, par, 1)), group)
                    layer2(p - 1, 16 * p, p + 1, group)
            last = PAIRS - 1
            layer1(last, 16 * last - 8, None, last // 2 - 1)
            layer2(last - 1, 16 * last, None, last // 2 - 1)
            layer2(last, 16 * last + 8, None)
            hidden1(last // 2)
            hidden2(last // 2)
            scores(last // 2)


def kernel(**inputs):
    import numpy as np
    import concourse.bacc as bacc
    from concourse.bass_utils import run_bass_kernel_spmd

    x = {k: np.asarray(v) for k, v in inputs.items()}
    tables = [x[f"tbl_{f}"] for f in range(FIELDS)]
    starts = np.cumsum([0] + [t.shape[0] for t in tables[:-1]]).astype(np.int32)
    pick = np.zeros((FIELDS, 3, SUMS, P), np.float32)
    m = np.arange(FIELDS)
    first, second = [], []
    for u in range(4):
        for i in range(4):
            h = (m + 4 * u + i + 1) % FIELDS
            pick[m, :, u, FIELDS * i + m] = 1.0
            pick[h, :, u, FIELDS * i + m] = 1.0
            first.append(m)
            second.append(h)
    pick[m, :, 4, m] = 1.0
    first, second = np.concatenate(first), np.concatenate(second)
    w0 = x["L0_rec_W0"]
    w0_ab = np.stack([w0[first, second], w0[second, first]]).reshape(2, 4, P, UNITS).transpose(2, 0, 1, 3)

    def product_weights(w):
        return w.reshape(TS, 4, SS, 32, UNITS).transpose(3, 1, 0, 2, 4).reshape(P, TS * SS * UNITS)

    arrays = {
        "ids": x["ids"].reshape(BATCH // QUADS, P).T,
        "base": np.tile(starts, QUADS).reshape(P, 1),
        "table": np.concatenate(tables, axis=0),
        "pick": pick.reshape(3 * FIELDS, SUMS * P),
        "w0_ab": w0_ab.reshape(P, 2, 4 * UNITS),
        "w0": w0,
        "w1": product_weights(x["L0_rec_W1"]),
        "w2": product_weights(x["L0_rec_W2"]),
        "dense": x["dense_ctx"].reshape(PAIRS, JS, QUADS, DIM).transpose(3, 0, 2, 1).reshape(DIM, BATCH),
        "wt1": x["W_top1"],
        "bt1": x["b_top1"].reshape(MLP1 // P, P).T,
        "wt2": x["W_top2"],
        "bt2": x["b_top2"].reshape(MLP2 // P, P).T,
        "wt3": x["W_top3"].reshape(MLP2 // P, P).T,
    }
    arrays = {k: np.ascontiguousarray(v) for k, v in arrays.items()}
    nc = bacc.Bacc("TRN2", target_bir_lowering=False, num_devices=1)
    args = [nc.dram_tensor(f"in_{k}", v.shape, mybir.dt.from_np(v.dtype), kind="ExternalInput").ap()
            for k, v in arrays.items()]
    out = nc.dram_tensor("out_score", (1, BATCH), F32, kind="ExternalOutput").ap()
    cin_tower(nc, *args, out)
    got = run_bass_kernel_spmd(nc, [{f"in_{k}": v for k, v in arrays.items()}], core_ids=[0]).results[0]["out_score"]
    return got.reshape(PAIRS, QUADS, JS).transpose(0, 2, 1).reshape(BATCH, 1)
```

```python
from contextlib import ExitStack

import concourse.bass as bass
from concourse import mybir

F32 = mybir.dt.float32
BF16 = mybir.dt.bfloat16
I32 = mybir.dt.int32
ALU = mybir.AluOpType
ACT = mybir.ActivationFunctionType
AXX = mybir.AxisListType.X

P = 128
BATCH, FIELDS, DIM, UNITS = 1024, 32, 16, 64
QUADS = 4
PAIRS = 16
JS = BATCH // PAIRS // QUADS
GCOLS = JS * DIM
CCOLS = GCOLS // 2
COLS = QUADS * GCOLS
HALF = COLS // 2
ROWS = HALF // DIM
SUMS = 4
SQ = 2 * SUMS
TS, SS = FIELDS // 4, UNITS // 32
RING = 4
BANKS = 2
GATHERED = 16 * JS // 2
AHEAD = 4
REPLICATED = 16 * 4
STACKED = 16 * QUADS
WARM_UP = 56
LOOPS = (PAIRS - 2) // 2
MLP1, MLP2 = 512, 256
GROUP = 2 * BATCH // PAIRS


def cin_tower(nc, ids, base, table, pick, w0_ab, w0, w1, w2, dense, wt1, bt1, wt2, bt2, wt3, out):
    ctx = ExitStack()
    with ctx:
        def sb(name, shape, dt=F32):
            return ctx.enter_context(nc.sbuf_tensor(name, shape, dt))

        def sem(name):
            return ctx.enter_context(nc.semaphore(name))

        ids_sb = sb("ids_sb", [P, BATCH // QUADS], I32)
        base_sb = sb("base_sb", [P, 1], I32)
        rows_sb = sb("rows_sb", [P, BATCH // QUADS], I32)
        emb = [sb(f"emb{b}", [P, 3, GCOLS]) for b in range(2)]
        stack = [sb(f"stack{b}", [3 * FIELDS, COLS]) for b in range(2)]
        xrep = [sb(f"xrep{b}", [P, TS, COLS]) for b in range(2)]
        x_dram = nc.dram_tensor("x_scratch", (2, FIELDS, COLS), F32, kind="Internal").ap()
        pick_sb = sb("pick_sb", [3 * FIELDS, SUMS * P], BF16)
        w0_sb = sb("w0_sb", [P, SUMS, UNITS])
        w0_own = sb("w0_own", [P, QUADS, UNITS])
        own = sb("own", [P, GCOLS])
        w1_sb = sb("w1_sb", [P, TS, SS, UNITS])
        w2_sb = sb("w2_sb", [P, TS, SS, UNITS])
        squares = sb("squares", [P, SUMS, COLS])
        prod = [sb(f"prod{r}", [P, SS, COLS]) for r in range(RING)]
        y = [sb(f"y{n}", [P, HALF]) for n in range(3)]
        yrep1 = [sb(f"yrep1_{b}", [P, SS, COLS]) for b in range(2)]
        yrep2 = [sb(f"yrep2_{b}", [P, SS, COLS]) for b in range(2)]
        zt = sb("zt", [P, 3, PAIRS, ROWS])
        pick_f = prod[0][0:3 * FIELDS, 0, 0:SUMS * P]
        w0_a = prod[1][:, 0, 0:4 * UNITS]
        w0_b = prod[1][:, 0, 4 * UNITS:8 * UNITS]
        w0_diag = prod[1][0:FIELDS, 1, 0:UNITS]
        w0_rsum = prod[1][0:FIELDS, 1, UNITS:2 * UNITS]
        w0_csum = prod[1][0:FIELDS, 1, 2 * UNITS:3 * UNITS]
        w0_rows = prod[2][0:FIELDS, :, :].rearrange("m s n -> m (s n)")
        w0_cols = prod[3][0:FIELDS, :, :].rearrange("m s n -> m (s n)")
        wt1_sb = sb("wt1_sb", [P, 2, MLP1])
        wt1_z2 = sb("wt1_z2", [P, MLP1])
        wt2_sb = sb("wt2_sb", [P, MLP1 // P, MLP2])
        wt3_sb = sb("wt3_sb", [P, MLP2 // P])
        bt1_sb = sb("bt1_sb", [P, MLP1 // P])
        bt2_sb = sb("bt2_sb", [P, MLP2 // P])
        feat = sb("feat", [P, 2, GROUP])
        h1 = sb("h1", [P, MLP1 // P, GROUP])
        h2 = sb("h2", [P, MLP2 // P, GROUP])
        score = sb("score", [1, BATCH])

        acc = [ctx.enter_context(nc.psum_tensor(f"acc{n}", [P, HALF], F32)) for n in range(3)]
        sums = [ctx.enter_context(nc.psum_tensor(f"sums{n}", [P, HALF], F32)) for n in range(BANKS)]

        h1_acc = ctx.enter_context(nc.psum_tensor("h1_acc", [P, MLP1 // P, GROUP], F32))
        h2_acc = ctx.enter_context(nc.psum_tensor("h2_acc", [P, 4, GROUP], F32))
        score_acc = ctx.enter_context(nc.psum_tensor("score_acc", [P, 4, GROUP], F32))

        h1_last = [bank[:, 0:GROUP] for bank in (acc[0], acc[1], sums[0], sums[1])]
        h2_last = [acc[2][:, 0:GROUP], h2_acc[:, 0, :]]

        ids_in = sem("ids_in")
        rows_ready = sem("rows_ready")
        gathered = [[sem(f"gathered{b}_{c}") for c in range(2)] for b in range(2)]
        split_first = [sem(f"split_first{c}") for c in range(2)]
        split_step = sem("split_step")
        stack_in = [sem(f"stack_in{b}") for b in range(2)]
        x_stored = [[sem(f"x_stored{b}_{c}") for c in range(2)] for b in range(2)]
        xrep_in = [[sem(f"xrep_in{b}_{t}") for t in range(TS)] for b in range(2)]
        stack_first = sem("stack_first")
        own_first = sem("own_first")
        layer0_first = sem("layer0_first")
        relued_first = sem("relued_first")
        xrep_first = [sem(f"xrep_first{t}") for t in range(AHEAD)]
        pick_in = sem("pick_in")
        pick_ready = sem("pick_ready")
        w0_in = sem("w0_in")
        w0_step = sem("w0_step")
        w12_in = sem("w12_in")
        mlp_in = sem("mlp_in")
        sums_ready = sem("sums_ready")
        own_squared = sem("own_squared")
        squared = sem("squared")
        layer0_done = sem("layer0_done")
        relued = [sem(f"relued{n}") for n in range(3)]
        reduced = [sem(f"reduced{n}") for n in range(3)]
        yrep1_in = [sem(f"yrep1_in{b}") for b in range(2)]
        yrep2_in = [sem(f"yrep2_in{b}") for b in range(2)]
        prod_ready = sem("prod_ready")
        prod_used = sem("prod_used")
        feat_in = sem("feat_in")
        h1_done = sem("h1_done")
        h1_ready = sem("h1_ready")
        h2_done = sem("h2_done")
        h2_ready = sem("h2_ready")
        score_done = sem("score_done")
        score_ready = sem("score_ready")
        out_stored = sem("out_stored")
        h1_parts = sem("h1_parts")
        h1_odd = sem("h1_odd")
        z2_left = sem("z2_left")
        h2_parts = sem("h2_parts")

        def uses(half, par, ahead):
            return half + (par + ahead) // 2 + 1

        def upper(x):
            return x.bitcast(BF16)[:, 1::2]

        def wait_gathered(engine, par, half):
            for c in range(2):
                engine.wait_ge(gathered[par][c], GATHERED * (half + 1))

        block = ctx.enter_context(nc.Block())

        @block.gpsimd
        def _(pool):
            pool.wait_ge(ids_in, 32)
            nc.gpsimd.tensor_tensor(rows_sb[:], ids_sb[:], base_sb[:].to_broadcast([P, BATCH // QUADS]),
                                    ALU.add).then_inc(rows_ready, 1)
            pool.wait_ge(rows_ready, 1)
            for p in range(PAIRS):
                par = p % 2
                if p >= 2:
                    for c in range(2):
                        pool.wait_ge(x_stored[par][c], 16 * (p // 2))
                    pool.wait_ge(stack_in[par], STACKED * (p // 2))
                    pool.wait_ge(own_squared, p - 1)
                for j in range(JS):
                    nc.gpsimd.indirect_dma_start(
                        emb[par][:, 0, j * DIM:j * DIM + DIM], None, table,
                        bass.IndirectOffsetOnAxis(ap=rows_sb[:, JS * p + j:JS * p + j + 1], axis=0),
                    ).then_inc(gathered[par][j // (JS // 2)], 16)
                if p >= 1:
                    wait_gathered(pool, par, p // 2)
                    for part in range(2):
                        if part == 1:
                            pool.wait_ge(split_step, 2 * p - 1)
                        nc.gpsimd.tensor_tensor(emb[par][:, part + 1, :], emb[par][:, part, :],
                                                upper(emb[par][:, part, :]), ALU.subtract).then_inc(split_step, 1)

        @block.sync
        def _(sp):
            def store_x(p, par, half):
                for c in range(2):
                    sp.wait_ge(gathered[par][c], GATHERED * (half + 1))
                    sp.nop(nofuse=True)
                    store_chunk(par, c)

            def store_chunk(par, c):
                sp.dma_start(x_dram[par][:, HALF * c:HALF * c + HALF].rearrange("m (q x) -> q m x", q=QUADS),
                             emb[par][:, 0, CCOLS * c:CCOLS * c + CCOLS]).then_inc(x_stored[par][c], 16)

            def load_stack(p, par, half):
                sp.wait_ge(split_step, 2 * p)
                for q in range(QUADS):
                    sp.dma_start(stack[par][:, GCOLS * q:GCOLS * q + GCOLS],
                                 emb[par][FIELDS * q:FIELDS * q + FIELDS, :, :]).then_inc(stack_in[par], 16)

            def load_xrep(p, par, half, before, some=range(TS)):
                for c in range(2):
                    sp.wait_ge(x_stored[par][c], 16 * (half + 1))
                sp.nop(nofuse=True)
                for t in some:
                    if before is not None:
                        sp.wait_ge(prod_ready, before + t + 1)
                    src = x_dram[par:par + 1, 4 * t:4 * t + 4, :].to_broadcast([32, 4, COLS])
                    sp.dma_start(xrep[par][:, t, :], src).then_inc(xrep_in[par][t], 16)

            def load_during(p, par, half):
                load_xrep(p + 1, 1 - par, half + par, 16 * p, range(0, RING))
                load_stack(p + 2, par, half + 1)
                store_x(p + 2, par, half + 1)
                load_xrep(p + 1, 1 - par, half + par, 16 * p, range(RING, TS))

            def load_first(c, arrived):
                sp.wait_ge(gathered[0][c], GATHERED)
                store_chunk(0, c)
                sp.wait_ge(split_first[c], 2)
                for q in range(QUADS):
                    at = GCOLS * q + CCOLS * c
                    sp.dma_start(stack[0][:, at:at + CCOLS],
                                 emb[0][FIELDS * q:FIELDS * q + FIELDS, :, CCOLS * c:CCOLS * c + CCOLS]
                                 ).then_inc(stack_in[0] if c else stack_first, 16)
                sp.wait_ge(x_stored[0][c], 16)
                for t in range(AHEAD):
                    src = x_dram[0:1, 4 * t:4 * t + 4, HALF * c:HALF * c + HALF].to_broadcast([32, 4, HALF])
                    sp.dma_start(xrep[0][:, t, HALF * c:HALF * c + HALF], src).then_inc(arrived[t], 16)

            def load_z01(g):
                for n in range(2):
                    for c in range(2):
                        sp.dma_start(feat[UNITS * n:UNITS * n + UNITS, 0, :].rearrange(
                            "k (p c r) -> k c p r", p=2, c=2)[:, c],
                            zt[UNITS * c:UNITS * c + UNITS, n, bass.ds(2 * g, 2), :]).then_inc(feat_in, 16)
                sp.dma_start(feat[UNITS:UNITS + DIM, 1, :], dense[:, bass.ds(g * GROUP, GROUP)]).then_inc(feat_in, 16)

            def load_z2(g):
                for c in range(2):
                    sp.dma_start(feat[0:UNITS, 1, :].rearrange("k (p c r) -> k c p r", p=2, c=2)[:, c],
                                 zt[UNITS * c:UNITS * c + UNITS, 2, bass.ds(2 * g, 2), :]).then_inc(feat_in, 16)

            def load_features(g):
                sp.wait_ge(reduced[2], 2 * g + 2)
                sp.nop(nofuse=True)
                if not (isinstance(g, int) and g < 1):
                    sp.wait_ge(h1_done, g)
                    sp.nop(nofuse=True)
                load_z01(g)
                load_z2(g)

            sp.dma_start(ids_sb[:], ids).then_inc(ids_in, 16)
            sp.dma_start(base_sb[:], base).then_inc(ids_in, 16)
            sp.dma_start(w0_a, w0_ab[:, 0, :]).then_inc(w0_in, 16)
            sp.dma_start(w0_b, w0_ab[:, 1, :]).then_inc(w0_in, 16)
            sp.dma_start(w0_diag, bass.AP(w0.tensor, w0.offset, [[(FIELDS + 1) * UNITS, FIELDS], [1, UNITS]])
                         ).then_inc(w0_in, 16)
            sp.dma_start(w0_rows, w0.rearrange("m h k -> m (h k)")).then_inc(w0_in, 16)
            sp.dma_start(w0_cols.rearrange("h (m k) -> h m k", k=UNITS), w0.rearrange("m h k -> h m k")
                         ).then_inc(w0_in, 16)
            load_first(0, xrep_first)
            load_first(1, xrep_in[0])
            load_xrep(0, 0, 0, None, range(AHEAD, 5))
            sp.wait_ge(yrep1_in[0], REPLICATED)
            load_xrep(0, 0, 0, None, range(5, TS))
            load_stack(1, 1, 0)
            store_x(1, 1, 0)
            load_xrep(1, 1, 0, None, range(0, 4))
            sp.wait_ge(yrep1_in[1], REPLICATED)
            load_xrep(1, 1, 0, None, range(4, 5))
            load_stack(2, 0, 1)
            load_xrep(1, 1, 0, None, range(5, TS))
            sp.wait_ge(prod_ready, TS)
            store_x(2, 0, 1)
            for p in (1, 2):
                load_during(p, p % 2, p // 2)
            with sp.Fori(1, LOOPS - 1) as i:
                for par in (1, 0):
                    p = 2 * i + 2 - par
                    half = i + 1 - par
                    load_during(p, par, half)
                    if par == 1:
                        load_features(i - 1)
            p = PAIRS - 3
            load_during(p, 1, p // 2)
            load_features(PAIRS // 2 - 3)
            p = PAIRS - 2
            load_xrep(p + 1, 1, p // 2, 16 * p)
            load_features(PAIRS // 2 - 2)
            g = PAIRS // 2 - 1
            sp.wait_ge(reduced[1], PAIRS)
            sp.wait_ge(h1_done, g)
            sp.dma_start(wt1_z2[UNITS:P, :], wt1[P:P + UNITS]).then_inc(feat_in, 16)
            for c in range(2):
                rows = slice(GROUP // 2 * c, GROUP // 2 * c + GROUP // 2)
                for n in range(2):
                    sp.dma_start(feat[UNITS * n:UNITS * n + UNITS, 0, rows],
                                 zt[UNITS * c:UNITS * c + UNITS, n, PAIRS - 2:PAIRS, :]).then_inc(feat_in, 16)
                sp.dma_start(feat[UNITS:UNITS + DIM, 1, rows], dense[:, BATCH - GROUP:BATCH].rearrange(
                    "k (p c r) -> k c p r", p=2, c=2)[:, c]).then_inc(feat_in, 16)
            sp.wait_ge(score_ready, PAIRS // 2)
            sp.dma_start(out, score[:]).then_inc(out_stored, 16)
            sp.wait_ge(out_stored, 16)

        @block.scalar
        def _(act):
            def replicate(dst, src, arrived, chunks=(0, 1)):
                pitch = src.ap[0][0]
                for s in range(SS):
                    for c in chunks:
                        act.dma_start(dst[:, s, HALF * c:HALF * c + HALF],
                                      bass.AP(src.tensor, src.offset + (UNITS * c + 32 * s) * pitch,
                                              [[pitch, 32], [0, 4], [1, HALF]])).then_inc(arrived, 16)

            def squares_of(p, par, half):
                act.wait_ge(layer0_done, p)
                wait_gathered(act, par, half)
                nc.scalar.activation(own[:], emb[par][:, 0, :], ACT.Square).then_inc(own_squared, 1)
                for i in range(SQ):
                    k, c = i // 2, i % 2
                    act.wait_ge(sums_ready, SQ * p + i + 1)
                    nc.scalar.activation(squares[:, k, HALF * c:HALF * c + HALF], sums[i % BANKS][:],
                                         ACT.Square).then_inc(squared, 1)

            def first_layer0(c):
                act.wait_ge(gathered[0][c], GATHERED)
                nc.scalar.activation(own[:, CCOLS * c:CCOLS * c + CCOLS], emb[0][:, 0, CCOLS * c:CCOLS * c + CCOLS],
                                     ACT.Square).then_inc(own_squared if c else own_first, 1)
                for k in range(SUMS):
                    i = SUMS * c + k
                    act.wait_ge(sums_ready, i + 1)
                    nc.scalar.activation(squares[:, k, HALF * c:HALF * c + HALF], sums[i % BANKS][:],
                                         ACT.Square).then_inc(squared, 1)
                act.wait_ge(layer0_done if c else layer0_first, 1)
                relued_c = relued[0] if c else relued_first
                half_y = y[0][UNITS * c:UNITS * c + UNITS, :]
                nc.scalar.activation(half_y, acc[0][UNITS * c:UNITS * c + UNITS, :], ACT.Relu).then_inc(relued_c, 1)
                act.wait_ge(relued_c, 1)
                if c:
                    act.wait_ge(yrep1_in[0], REPLICATED // 2)
                replicate(yrep1[0], y[0][:], yrep1_in[0], (c,))

            def relu0(p, par, half):
                act.wait_ge(layer0_done, p + 1)
                act.wait_ge(reduced[0], p)
                act.wait_ge(yrep1_in[1 - par], REPLICATED * uses(half, par, -1))
                nc.scalar.activation(y[0][:], acc[0][:], ACT.Relu).then_inc(relued[0], 1)
                act.wait_ge(relued[0], p + 1)
                if not (isinstance(p, int) and p < 2):
                    act.wait_ge(prod_ready, 16 * (p - 2) if not (isinstance(p, int) and p == 2) else TS)
                replicate(yrep1[par], y[0][:], yrep1_in[par])

            def relu1(p, par, half):
                act.wait_ge(prod_used, 16 * p if not (isinstance(p, int) and p < 1) else TS)
                if not (isinstance(p, int) and p < 1):
                    act.wait_ge(reduced[1], p)
                    act.wait_ge(yrep2_in[1 - par], REPLICATED * uses(half, par, -1))
                nc.scalar.activation(y[1][:], acc[1][:], ACT.Relu).then_inc(relued[1], 1)
                act.wait_ge(relued[1], p + 1)
                if not (isinstance(p, int) and p < 2):
                    act.wait_ge(prod_ready, 16 * p - 8)
                replicate(yrep2[par], y[1][:], yrep2_in[par])

            def relu2(p, used):
                act.wait_ge(prod_used, used)
                if not (isinstance(p, int) and p < 1):
                    act.wait_ge(reduced[2], p)
                nc.scalar.activation(y[2][:], acc[2][:], ACT.Relu).then_inc(relued[2], 1)

            def rectify_h1(g):
                if not (isinstance(g, int) and g < 1):
                    act.wait_ge(h2_done, g)
                act.wait_ge(h1_done, g + 1)
                for m in range(MLP1 // P):
                    nc.scalar.activation(h1[:, m, :], h1_acc[:, m, :], ACT.Relu,
                                         bias=bt1_sb[:, m:m + 1]).then_inc(h1_ready, 1)

            def rectify_h2(g):
                if not (isinstance(g, int) and g < 1):
                    act.wait_ge(score_done, g)
                act.wait_ge(h2_done, g + 1)
                for m in range(MLP2 // P):
                    nc.scalar.activation(h2[:, m, :], h2_acc[:, m, :], ACT.Relu,
                                         bias=bt2_sb[:, m:m + 1]).then_inc(h2_ready, 1)

            def keep_score(g):
                act.wait_ge(score_done, g + 1)
                nc.scalar.copy(score[:, bass.ds(g * GROUP, GROUP)], score_acc[0:1, 0, :]).then_inc(score_ready, 1)

            act.dma_start(pick_f, pick).then_inc(pick_in, 16)
            act.dma_start(w1_sb[:].rearrange("p t s k -> p (t s k)"), w1).then_inc(w12_in, 16)
            act.dma_start(w2_sb[:].rearrange("p t s k -> p (t s k)"), w2).then_inc(w12_in, 16)
            act.dma_start(wt1_sb[:, 0, :], wt1[0:P]).then_inc(mlp_in, 16)
            act.dma_start(wt1_sb[0:UNITS + DIM, 1, :], wt1[P:P + UNITS + DIM]).then_inc(mlp_in, 16)
            act.dma_start(wt2_sb[:], wt2.rearrange("(t p) n -> p t n", p=P)).then_inc(mlp_in, 16)
            act.dma_start(wt3_sb[:], wt3).then_inc(mlp_in, 16)
            act.dma_start(bt1_sb[:], bt1).then_inc(mlp_in, 16)
            act.dma_start(bt2_sb[:], bt2).then_inc(mlp_in, 16)
            for c in range(2):
                first_layer0(c)
            squares_of(1, 1, 0)
            relu0(1, 1, 0)
            relu1(0, 0, 0)
            for p in (1, 2):
                squares_of(p + 1, 1 - p % 2, (p + 1) // 2)
                relu0(p + 1, 1 - p % 2, (p + 1) // 2)
                relu1(p, p % 2, p // 2)
                relu2(p - 1, 16 * p + 8)
            act.wait_ge(mlp_in, 16 * 6)
            with act.Fori(1, LOOPS) as i:
                for par in (1, 0):
                    p = 2 * i + 2 - par
                    half = i + 1 - par
                    squares_of(p + 1, 1 - par, half + par)
                    relu0(p + 1, 1 - par, half + par)
                    relu1(p, par, half)
                    if par == 0:
                        rectify_h1(i - 1)
                        rectify_h2(i - 1)
                        keep_score(i - 1)
                    relu2(p - 1, 16 * p + 8)
            last = PAIRS - 1
            g = PAIRS // 2 - 2
            relu1(last, 1, last // 2)
            rectify_h1(g)
            rectify_h2(g)
            keep_score(g)
            relu2(last - 1, 16 * last + 8)
            relu2(last, 16 * last + 16)
            for m in range(0, MLP1 // P, 2):
                act.wait_ge(h1_parts, m + 1)
                nc.scalar.activation(h1[:, m, :], h1_last[m], ACT.Relu, bias=bt1_sb[:, m:m + 1]).then_inc(h1_ready, 1)
            for m in range(MLP2 // P):
                act.wait_ge(h2_parts, m + 1)
                nc.scalar.activation(h2[:, m, :], h2_last[m], ACT.Relu, bias=bt2_sb[:, m:m + 1]).then_inc(h2_ready, 1)
            act.wait_ge(score_done, PAIRS // 2)
            nc.scalar.copy(score[:, BATCH - GROUP:BATCH].rearrange("o (p c r) -> o c p r", p=2, c=2),
                           score_acc[0:1, 0, :].rearrange("o (c p r) -> o c p r", p=2, c=2)).then_inc(score_ready, 1)

        @block.vector
        def _(dve):
            def products(at, t, xr, yr):
                if not (isinstance(at, int) and at < RING):
                    dve.wait_ge(prod_used, at - RING + 1)
                nc.vector.tensor_tensor(prod[t % RING][:], xr[:, t:t + 1, :].to_broadcast([P, SS, COLS]), yr[:],
                                        ALU.mult).then_inc(prod_ready, 1)

            def split_chunk(c):
                for part in range(2):
                    if part == 0:
                        dve.wait_ge(gathered[0][c], GATHERED)
                    else:
                        dve.wait_ge(split_first[c], 1)
                    x_c = emb[0][:, part, CCOLS * c:CCOLS * c + CCOLS]
                    nc.vector.tensor_tensor(emb[0][:, part + 1, CCOLS * c:CCOLS * c + CCOLS], x_c, upper(x_c),
                                            ALU.subtract).then_inc(split_first[c], 1)

            def products_ahead(c):
                dve.wait_ge(yrep1_in[0], REPLICATED // 2 * (c + 1))
                for t in range(AHEAD):
                    dve.wait_ge(xrep_in[0][t] if c else xrep_first[t], 16)
                    x_c = xrep[0][:, t:t + 1, HALF * c:HALF * c + HALF].to_broadcast([P, SS, HALF])
                    made = nc.vector.tensor_tensor(prod[t][:, :, HALF * c:HALF * c + HALF], x_c,
                                                   yrep1[0][:, :, HALF * c:HALF * c + HALF], ALU.mult)
                    if c:
                        made.then_inc(prod_ready, 1)

            def reduce_d(n, p):
                dve.wait_ge(relued[n], p + 1)
                nc.vector.tensor_reduce(zt[:, n, bass.ds(p, 1), :].rearrange("u o r -> u (o r)"),
                                        y[n][:].rearrange("p (r d) -> p r d", d=DIM), AXX,
                                        ALU.add).then_inc(reduced[n], 1)

            def layer1(p, par, half, at, y2=True, y1=None, some=range(TS)):
                dve.wait_ge(yrep1_in[par], REPLICATED * (half + 1))
                for t in some:
                    dve.wait_ge(xrep_in[par][t], 16 * (half + 1))
                    products(at + t, t, xrep[par], yrep1[par])
                    if t == 4 and y2:
                        reduce_d(2, p - 2)
                    if t == 4 and y1 is not None:
                        reduce_d(1, y1)

            def layer2(p, par, half, at, y1, y0):
                dve.wait_ge(yrep2_in[par], REPLICATED * (half + 1))
                for t in range(TS):
                    products(at + t, t, xrep[par], yrep2[par])
                    if t == 3 and y0 is not None:
                        reduce_d(0, y0)
                    if t == 6 and y1 is not None:
                        reduce_d(1, y1)

            dve.wait_ge(pick_in, 16)
            nc.vector.tensor_copy(pick_sb[:], pick_f).then_inc(pick_ready, 1)
            dve.wait_ge(w0_in, 16 * 5)
            nc.vector.memset(w0_own[:], 0.0).then_inc(w0_step, 1)
            pairs_w = w0_sb[:].rearrange("p u k -> p (u k)")
            nc.vector.tensor_tensor(w0_a, w0_a, w0_b, ALU.add).then_inc(w0_step, 1)
            nc.vector.tensor_reduce(w0_rsum, w0_rows.rearrange("m (h k) -> m k h", k=UNITS), AXX,
                                    ALU.add).then_inc(w0_step, 1)
            split_chunk(0)
            nc.vector.tensor_reduce(w0_csum, w0_cols.rearrange("h (m k) -> h k m", k=UNITS), AXX,
                                    ALU.add).then_inc(w0_step, 1)
            dve.wait_ge(w0_step, 4)
            nc.vector.tensor_scalar_mul(pairs_w, w0_a, 0.5).then_inc(w0_step, 1)
            nc.vector.tensor_tensor(w0_rsum, w0_rsum, w0_csum, ALU.add).then_inc(w0_step, 1)
            dve.wait_ge(w0_step, 6)
            nc.vector.tensor_scalar_mul(w0_sb[96:128, 3, :], w0_sb[96:128, 3, :], 0.5).then_inc(w0_step, 1)
            nc.vector.tensor_scalar_mul(w0_rsum, w0_rsum, -0.5).then_inc(w0_step, 1)
            dve.wait_ge(w0_step, 8)
            nc.vector.scalar_tensor_tensor(out=w0_diag, in0=w0_diag, scalar=2.0, in1=w0_rsum, op0=ALU.mult,
                                           op1=ALU.add).then_inc(w0_step, 1)
            dve.wait_ge(w0_step, 9)
            for q in range(QUADS):
                nc.vector.tensor_copy(w0_own[FIELDS * q:FIELDS * q + FIELDS, q, :], w0_diag).then_inc(w0_step, 1)
            dve.wait_ge(w0_step, 13)
            split_chunk(1)
            products_ahead(0)
            reduce_d(0, 0)
            products_ahead(1)
            layer1(0, 0, 0, 0, y2=False, some=range(AHEAD, TS))
            reduce_d(0, 1)
            layer1(1, 1, 0, TS, y2=False, y1=0)
            layer2(0, 0, 0, 2 * TS, 1, 2)
            layer1(2, 0, 1, 3 * TS)
            layer2(1, 1, 0, 4 * TS, 2, 3)
            with dve.Fori(1, LOOPS) as i:
                for par in (1, 0):
                    p = 2 * i + 2 - par
                    half = i + 1 - par
                    layer1(p, par, half, 16 * p - 8)
                    layer2(p - 1, 1 - par, half + par - 1, 16 * p, p, p + 1)
            last = PAIRS - 1
            layer1(last, 1, last // 2, 16 * last - 8)
            layer2(last - 1, 0, last // 2, 16 * last, last, None)
            dve.wait_ge(yrep2_in[1], REPLICATED * (last // 2 + 1))
            for t in range(TS - 1):
                products(16 * last + 8 + t, t, xrep[1], yrep2[1])
                if t == 2:
                    reduce_d(2, last - 1)
            dve.wait_ge(prod_used, 16 * PAIRS - RING)
            for s in range(SS):
                nc.vector.tensor_tensor(prod[(TS - 1) % RING][:, s, :], xrep[1][:, TS - 1, :], yrep2[1][:, s, :],
                                        ALU.mult).then_inc(prod_ready, 1)
            reduce_d(2, last)
            for m in range(1, MLP1 // P, 2):
                dve.wait_ge(h1_parts, m + 1)
                nc.vector.tensor_scalar(h1[:, m, :], h1_last[m], bt1_sb[:, m:m + 1], 0.0, ALU.add,
                                        ALU.max).then_inc(h1_odd, 1)

        @block.tensor
        def _(pe):
            def warm_up(bank, count):
                with pe.Fori(0, count // 4):
                    for _ in range(4):
                        nc.tensor.matmul(bank, pick_sb[:, 0:P], pick_sb[:, 0:HALF], start=True, stop=True)

            def chunk_columns(tile, c):
                return tile.rearrange("m (q c x) -> m c q x", q=QUADS, c=2)[:, c]

            def pair_sum(p, par, k, c, i):
                if not (isinstance(p, int) and SQ * p + i < BANKS):
                    pe.wait_ge(squared, SQ * p + i - BANKS + 1)
                nc.tensor.matmul(sums[i % BANKS][:].rearrange("p (q x) -> p q x", q=QUADS),
                                 pick_sb[:, P * k:P * k + P], chunk_columns(upper(stack[par][:]), c), start=True,
                                 stop=True).then_inc(sums_ready, 1)

            def pair_sums(p, par, k):
                for c in range(2):
                    pair_sum(p, par, k, c, 2 * k + c)

            def weigh(k, c):
                nc.tensor.matmul(acc[0][UNITS * c:UNITS * c + UNITS, :], w0_sb[:, k, :],
                                 squares[:, k, HALF * c:HALF * c + HALF], start=(k == 0), stop=False)

            def weigh_own(q, c):
                return nc.tensor.matmul(acc[0][UNITS * c:UNITS * c + UNITS, CCOLS * q:CCOLS * q + CCOLS],
                                        w0_own[:, q, :], own[:, CCOLS * c:CCOLS * c + CCOLS], start=False,
                                        stop=(q == QUADS - 1))

            def layer0(p, k):
                if k == 0:
                    pe.wait_ge(relued[0], p)
                if k < SUMS:
                    pe.wait_ge(squared, SQ * p + 2 * k + 2)
                    for c in range(2):
                        weigh(k, c)
                else:
                    pe.wait_ge(own_squared, p + 1)
                    for q in range(QUADS):
                        for c in range(2):
                            mm = weigh_own(q, c)
                    mm.then_inc(layer0_done, 1)

            def first_layer0(c):
                pe.wait_ge(stack_in[0] if c else stack_first, STACKED)
                for k in range(SUMS + 1):
                    if k < SUMS:
                        pair_sum(0, 0, k, c, SUMS * c + k)
                    if k == 0 and c == 0:
                        pe.wait_ge(w0_step, 13)
                    if k:
                        pe.wait_ge(squared, SUMS * c + k)
                        weigh(k - 1, c)
                pe.wait_ge(own_squared if c else own_first, 1)
                for q in range(QUADS):
                    mm = weigh_own(q, c)
                mm.then_inc(layer0_done if c else layer0_first, 1)

            def contract(at, t, w, to, halves=False):
                pe.wait_ge(prod_ready, at + t + 1)
                for s in range(SS):
                    if halves and s == 1:
                        pe.wait_ge(prod_ready, at + t + 2)
                    for c in range(2):
                        mm = nc.tensor.matmul(to[UNITS * c:UNITS * c + UNITS, :], w[:, t, s, :],
                                              prod[t % RING][:, s, HALF * c:HALF * c + HALF],
                                              start=(t == 0 and s == 0), stop=(t == TS - 1 and s == SS - 1))
                    if s == SS - 1:
                        mm.then_inc(prod_used, 1)

            def hidden1(g):
                pe.wait_ge(feat_in, 16 * 7 * (g + 1))
                for m in range(MLP1 // P):
                    for k, n in ((0, P), (1, UNITS + DIM)):
                        mm = nc.tensor.matmul(h1_acc[:, m, :], wt1_sb[0:n, k, P * m:P * m + P], feat[0:n, k, :],
                                              start=(k == 0), stop=(k == 1))
                mm.then_inc(h1_done, 1)

            def hidden2(g):
                pe.wait_ge(h1_ready, MLP1 // P * (g + 1))
                for m in range(MLP2 // P):
                    for k in range(MLP1 // P):
                        mm = nc.tensor.matmul(h2_acc[:, m, :], wt2_sb[:, k, P * m:P * m + P], h1[:, k, :],
                                              start=(k == 0), stop=(k == MLP1 // P - 1))
                mm.then_inc(h2_done, 1)

            def scores(g):
                pe.wait_ge(h2_ready, MLP2 // P * (g + 1))
                if not (isinstance(g, int) and g < 1):
                    pe.wait_ge(score_ready, g)
                for k in range(MLP2 // P):
                    mm = nc.tensor.matmul(score_acc[0:1, 0, :], wt3_sb[:, k:k + 1], h2[:, k, :], start=(k == 0),
                                          stop=(k == MLP2 // P - 1))
                mm.then_inc(score_done, 1)

            def layer1(p, at, par_next, sums_at, layer0_at):
                if not (isinstance(p, int) and p < 1):
                    pe.wait_ge(relued[1], p)
                for t in range(TS):
                    contract(at, t, w1_sb, acc[1])
                    if sums_at[t] and sums_at[t][0] == 0:
                        pe.wait_ge(stack_in[par_next[0]], STACKED * par_next[1])
                    for k in sums_at[t]:
                        pair_sums(p + 1, par_next[0], k)
                    for k in layer0_at[t]:
                        layer0(p + 1, k)

            def mlp_last():
                g = PAIRS // 2 - 1
                pe.wait_ge(feat_in, 16 * 7 * (g + 1))
                pe.wait_ge(relued[0], PAIRS)
                pe.wait_ge(relued[1], PAIRS)
                pe.wait_ge(squared, SQ * PAIRS)
                for m in range(MLP1 // P):
                    nc.tensor.matmul(h1_last[m], wt1_sb[:, 0, P * m:P * m + P], feat[:, 0, :], start=True, stop=False)
                    nc.tensor.matmul(h1_last[m], wt1_sb[UNITS:UNITS + DIM, 1, P * m:P * m + P],
                                     feat[UNITS:UNITS + DIM, 1, :], start=False, stop=False)
                pe.wait_ge(reduced[2], PAIRS)
                for c in range(2):
                    w_z2 = wt1_z2[UNITS:P, :] if c else wt1_sb[0:UNITS, 1, :]
                    for m in range(MLP1 // P):
                        if c:
                            pe.wait_ge(z2_left, m + 1)
                        mm = nc.tensor.matmul(h1_last[m][:, GROUP // 2 * c:GROUP // 2 * c + GROUP // 2],
                                              w_z2[:, P * m:P * m + P],
                                              zt[UNITS * c:UNITS * c + UNITS, 2, PAIRS - 2:PAIRS, :], start=False,
                                              stop=(c == 1))
                        mm.then_inc(h1_parts if c else z2_left, 1)
                pe.wait_ge(relued[2], PAIRS)
                pe.wait_ge(h2_ready, MLP2 // P * g)
                for k in range(MLP1 // P):
                    if k % 2 == 0:
                        pe.wait_ge(h1_ready, MLP1 // P * g + k // 2 + 1)
                    else:
                        pe.wait_ge(h1_odd, k // 2 + 1)
                    for m in range(MLP2 // P):
                        mm = nc.tensor.matmul(h2_last[m], wt2_sb[:, k, P * m:P * m + P], h1[:, k, :],
                                              start=(k == 0), stop=(k == MLP1 // P - 1))
                        if k == MLP1 // P - 1:
                            mm.then_inc(h2_parts, 1)
                pe.wait_ge(score_ready, g)
                for k in range(MLP2 // P):
                    pe.wait_ge(h2_ready, MLP2 // P * g + k + 1)
                    mm = nc.tensor.matmul(score_acc[0:1, 0, :], wt3_sb[:, k:k + 1], h2[:, k, :], start=(k == 0),
                                          stop=(k == MLP2 // P - 1))
                mm.then_inc(score_done, 1)

            def layer2(p, at, group=None):
                if not (isinstance(p, int) and p < 1):
                    pe.wait_ge(relued[2], p)
                for t in range(TS):
                    contract(at, t, w2_sb, acc[2])
                    if t == 1 and group is not None:
                        hidden1(group)
                    if t == 4 and group is not None:
                        hidden2(group)
                    if t == 6 and group is not None:
                        scores(group)

            pe.wait_ge(pick_ready, 1)
            warm_up(acc[1][:], WARM_UP)
            for c in range(2):
                first_layer0(c)
            pe.wait_ge(w12_in, 32)
            layer1(0, 0, (1, 1), ((), (), (0, 1), (2, 3), (), (), (), ()),
                   ((), (), (), (0, 1, 2, 3, 4), (), (), (), ()))
            sums_at = ((0,), (1,), (2,), (3,), (), (), (), ())
            layer0_at = ((), (), (0,), (1,), (2,), (3,), (4,), ())
            layer1(1, TS, (0, 2), ((), (), (), (0,), (1,), (2,), (3,), ()), ((), (), (), (), (), (0,), (1,), (2,3,4)))
            layer2(0, 2 * TS)
            layer1(2, 3 * TS, (1, 2), sums_at, layer0_at)
            layer2(1, 4 * TS)
            pe.wait_ge(mlp_in, 16 * 6)
            with pe.Fori(1, LOOPS) as i:
                for par in (1, 0):
                    p = 2 * i + 2 - par
                    half = i + 1 - par
                    group = i - 1 if par == 0 else None
                    layer1(p, 16 * p - 8, (1 - par, uses(half, par, 1)), sums_at, layer0_at)
                    layer2(p - 1, 16 * p, group)
            last = PAIRS - 1
            layer1(last, 16 * last - 8, None, [()] * TS, [()] * TS)
            layer2(last - 1, 16 * last, last // 2 - 1)
            pe.wait_ge(relued[2], last)
            for t in range(TS):
                contract(16 * last + 8, t, w2_sb, acc[2], halves=(t == TS - 1))
            mlp_last()


def kernel(**inputs):
    import numpy as np
    import concourse.bacc as bacc
    from concourse.bass_utils import run_bass_kernel_spmd

    x = {k: np.asarray(v) for k, v in inputs.items()}
    tables = [x[f"tbl_{f}"] for f in range(FIELDS)]
    starts = np.cumsum([0] + [t.shape[0] for t in tables[:-1]]).astype(np.int32)
    pick = np.zeros((FIELDS, 3, SUMS, P), np.float32)
    m = np.arange(FIELDS)
    first, second = [], []
    for u in range(4):
        for i in range(4):
            h = (m + 4 * u + i + 1) % FIELDS
            pick[m, :, u, FIELDS * i + m] = 1.0
            pick[h, :, u, FIELDS * i + m] = 1.0
            first.append(m)
            second.append(h)
    first, second = np.concatenate(first), np.concatenate(second)
    w0 = x["L0_rec_W0"]
    w0_ab = np.stack([w0[first, second], w0[second, first]]).reshape(2, 4, P, UNITS).transpose(2, 0, 1, 3)

    def product_weights(w):
        return w.reshape(TS, 4, SS, 32, UNITS).transpose(3, 1, 0, 2, 4).reshape(P, TS * SS * UNITS)

    arrays = {
        "ids": x["ids"].reshape(BATCH // QUADS, P).T,
        "base": np.tile(starts, QUADS).reshape(P, 1),
        "table": np.concatenate(tables, axis=0),
        "pick": pick.reshape(3 * FIELDS, SUMS * P),
        "w0_ab": w0_ab.reshape(P, 2, 4 * UNITS),
        "w0": w0,
        "w1": product_weights(x["L0_rec_W1"]),
        "w2": product_weights(x["L0_rec_W2"]),
        "dense": x["dense_ctx"].reshape(PAIRS, 2, JS // 2, QUADS, DIM).transpose(4, 0, 1, 3, 2).reshape(DIM, BATCH),
        "wt1": x["W_top1"],
        "bt1": x["b_top1"].reshape(MLP1 // P, P).T,
        "wt2": x["W_top2"],
        "bt2": x["b_top2"].reshape(MLP2 // P, P).T,
        "wt3": x["W_top3"].reshape(MLP2 // P, P).T,
    }
    arrays = {k: np.ascontiguousarray(v) for k, v in arrays.items()}
    nc = bacc.Bacc("TRN2", target_bir_lowering=False, num_devices=1)
    args = [nc.dram_tensor(f"in_{k}", v.shape, mybir.dt.from_np(v.dtype), kind="ExternalInput").ap()
            for k, v in arrays.items()]
    out = nc.dram_tensor("out_score", (1, BATCH), F32, kind="ExternalOutput").ap()
    cin_tower(nc, *args, out)
    got = run_bass_kernel_spmd(nc, [{f"in_{k}": v for k, v in arrays.items()}], core_ids=[0]).results[0]["out_score"]
    return got.reshape(PAIRS, 2, QUADS, JS // 2).transpose(0, 1, 3, 2).reshape(BATCH, 1)
```
